# Optimizing a Trainium2 kernel written in Bass

```python
import numpy as np
import jax
import jax.numpy as jnp

def _softmax(x, axis=-1):
    return jax.nn.softmax(x, axis=axis)

def _gelu(x):
    return jax.nn.gelu(x, approximate=True)

def _silu(x):
    return jax.nn.silu(x)

def _sigmoid(x):
    return jax.nn.sigmoid(x)

def _layernorm(x, axis=-1, eps=1e-05):
    m = jnp.mean(x, axis=axis, keepdims=True)
    v = jnp.var(x, axis=axis, keepdims=True)
    return (x - m) / jnp.sqrt(v + eps)

def _scatter_add(tgt, idx, src, axis=0):
    return tgt.at[idx].add(src)

def _segment_sum(src, seg, n):
    return jax.ops.segment_sum(src, seg, n)
kernel_name = 'mk_macaron_d1_jaxref_r8_245403'

def setup_inputs(seed: int=0):
    np.random.seed(seed)
    _w = jnp.asarray

    def _L0_attn_setup():
        import jax, jax.numpy as jnp
        import numpy as np
        HIDDEN = 128
        N_HEADS = 16
        D_HEAD = HIDDEN // N_HEADS

        def _rope(q, k):
            B, H, N, d = q.shape
            inv_freq = 1.0 / 10000.0 ** (jnp.arange(0, d, 2, dtype=jnp.float32) / d)
            pos = jnp.arange(N, dtype=jnp.float32)
            thetas = pos[:, None] * inv_freq[None, :]
            cos, sin = (jnp.cos(thetas), jnp.sin(thetas))

            def rot(x):
                xp = x.reshape(B, H, N, d // 2, 2)
                xx, xy = (xp[..., 0], xp[..., 1])
                rx = xx * cos - xy * sin
                ry = xx * sin + xy * cos
                return jnp.stack([rx, ry], axis=-1).reshape(B, H, N, d)
            return (rot(q), rot(k))
        key = jax.random.key(seed)
        ks = jax.random.split(key, 9)
        B, N, Hd = (4, 256, HIDDEN)
        s = 1.0 / np.sqrt(Hd)
        return {'x': jax.random.normal(ks[0], (B, N, Hd), jnp.float32), 'Wq': jax.random.normal(ks[1], (Hd, Hd), jnp.float32) * s, 'bq': jax.random.normal(ks[2], (Hd,), jnp.float32) * 0.02, 'Wk': jax.random.normal(ks[3], (Hd, Hd), jnp.float32) * s, 'bk': jax.random.normal(ks[4], (Hd,), jnp.float32) * 0.02, 'Wv': jax.random.normal(ks[5], (Hd, Hd), jnp.float32) * s, 'bv': jax.random.normal(ks[6], (Hd,), jnp.float32) * 0.02, 'Wo': jax.random.normal(ks[7], (Hd, Hd), jnp.float32) * s, 'bo': jax.random.normal(ks[8], (Hd,), jnp.float32) * 0.02}
    _L0_attn_in = _L0_attn_setup()

    def _L0_ffn_setup():
        import jax, jax.numpy as jnp
        import numpy as np
        EPS = 1e-05

        def _quantize(W):
            gamma = jnp.mean(jnp.abs(W))
            return jnp.clip(jnp.round(W / (gamma + EPS)), -1.0, 1.0)
        key = jax.random.key(seed)
        k_x, k_w1, k_b1, k_w2, k_b2 = jax.random.split(key, 5)
        n_embd = 128
        d_ff = 4 * n_embd
        B, S = (4, 512)
        bound1 = 1.0 / np.sqrt(n_embd)
        bound2 = 1.0 / np.sqrt(d_ff)
        x = jax.random.normal(k_x, (B, S, n_embd), dtype=jnp.float32)
        W1 = jax.random.uniform(k_w1, (d_ff, n_embd), jnp.float32, -bound1, bound1)
        b1 = jax.random.uniform(k_b1, (d_ff,), jnp.float32, -bound1, bound1)
        W2 = jax.random.uniform(k_w2, (n_embd, d_ff), jnp.float32, -bound2, bound2)
        b2 = jax.random.uniform(k_b2, (n_embd,), jnp.float32, -bound2, bound2)
        return {'x': x, 'W1': W1, 'b1': b1, 'W2': W2, 'b2': b2}
    _L0_ffn_in = _L0_ffn_setup()
    _d = {'L0_attn_x': _L0_attn_in['x'], 'L0_attn_Wq': _L0_attn_in['Wq'], 'L0_attn_bq': _L0_attn_in['bq'], 'L0_attn_Wk': _L0_attn_in['Wk'], 'L0_attn_bk': _L0_attn_in['bk'], 'L0_attn_Wv': _L0_attn_in['Wv'], 'L0_attn_bv': _L0_attn_in['bv'], 'L0_attn_Wo': _L0_attn_in['Wo'], 'L0_attn_bo': _L0_attn_in['bo'], 'L0_ffn_W1': _L0_ffn_in['W1'], 'L0_ffn_b1': _L0_ffn_in['b1'], 'L0_ffn_W2': _L0_ffn_in['W2'], 'L0_ffn_b2': _L0_ffn_in['b2']}
    _x0 = _d['L0_attn_x']
    _d['L0_attn_x'] = jax.random.normal(jax.random.fold_in(jax.random.key(seed), 1), (8, 512, 128), dtype=_x0.dtype)
    del _x0
    return _d

def reference(L0_attn_x, L0_attn_Wq, L0_attn_bq, L0_attn_Wk, L0_attn_bk, L0_attn_Wv, L0_attn_bv, L0_attn_Wo, L0_attn_bo, L0_ffn_W1, L0_ffn_b1, L0_ffn_W2, L0_ffn_b2):

    def _L0_attn_ref(x, Wq, bq, Wk, bk, Wv, bv, Wo, bo):
        import jax, jax.numpy as jnp
        import numpy as np
        HIDDEN = 128
        N_HEADS = 16
        D_HEAD = HIDDEN // N_HEADS

        def _rope(q, k):
            B, H, N, d = q.shape
            inv_freq = 1.0 / 10000.0 ** (jnp.arange(0, d, 2, dtype=jnp.float32) / d)
            pos = jnp.arange(N, dtype=jnp.float32)
            thetas = pos[:, None] * inv_freq[None, :]
            cos, sin = (jnp.cos(thetas), jnp.sin(thetas))

            def rot(x):
                xp = x.reshape(B, H, N, d // 2, 2)
                xx, xy = (xp[..., 0], xp[..., 1])
                rx = xx * cos - xy * sin
                ry = xx * sin + xy * cos
                return jnp.stack([rx, ry], axis=-1).reshape(B, H, N, d)
            return (rot(q), rot(k))
        B, N, _ = x.shape
        H, d = (N_HEADS, D_HEAD)
        q = (x @ Wq.T + bq).reshape(B, N, H, d).transpose(0, 2, 1, 3)
        k = (x @ Wk.T + bk).reshape(B, N, H, d).transpose(0, 2, 1, 3)
        v = (x @ Wv.T + bv).reshape(B, N, H, d).transpose(0, 2, 1, 3)
        q, k = _rope(q, k)
        scores = jnp.einsum('bhnd,bhmd->bhnm', q, k) / jnp.sqrt(jnp.asarray(d, x.dtype))
        attn = jax.nn.softmax(scores, axis=-1)
        out = jnp.einsum('bhnm,bhmd->bhnd', attn, v)
        out = out.transpose(0, 2, 1, 3).reshape(B, N, H * d)
        return out @ Wo.T + bo

    def _L0_ffn_ref(x, W1, b1, W2, b2):
        import jax, jax.numpy as jnp
        import numpy as np
        EPS = 1e-05

        def _quantize(W):
            gamma = jnp.mean(jnp.abs(W))
            return jnp.clip(jnp.round(W / (gamma + EPS)), -1.0, 1.0)
        Wq1 = _quantize(W1)
        Wq2 = _quantize(W2)
        h = jax.nn.relu(jnp.einsum('bsd,fd->bsf', x, Wq1) + b1)
        out = jnp.einsum('bsf,df->bsd', h, Wq2) + b2
        return out
    x = L0_attn_x
    x = x + 0.5 * _L0_ffn_ref(_layernorm(x, axis=-1), L0_ffn_W1, L0_ffn_b1, L0_ffn_W2, L0_ffn_b2)
    x = x + _L0_attn_ref(_layernorm(x, axis=-1), L0_attn_Wq, L0_attn_bq, L0_attn_Wk, L0_attn_bk, L0_attn_Wv, L0_attn_bv, L0_attn_Wo, L0_attn_bo)
    x = x + 0.5 * _L0_ffn_ref(_layernorm(x, axis=-1), L0_ffn_W1, L0_ffn_b1, L0_ffn_W2, L0_ffn_b2)
    return x

_drawn_inputs = setup_inputs


def setup_inputs(seed=0):
    import zlib

    import numpy as np

    out = dict(_drawn_inputs(seed))
    spreads = {}
    factors = {'L0_attn_Wq': 8.0,
     'L0_attn_bq': 8.0,
     'L0_attn_Wk': 8.0,
     'L0_attn_bk': 8.0,
     'L0_attn_Wv': 7.37,
     'L0_attn_bv': 33.914,
     'L0_attn_Wo': 8.0,
     'L0_attn_bo': 200.0,
     'L0_ffn_b1': 8.0,
     'L0_ffn_b2': 59.625}
    for name, (base, spread) in spreads.items():
        noise = np.random.default_rng([zlib.crc32(name.encode()), seed]).standard_normal(out[name].shape)
        drawn = base * np.exp(spread * noise) if base else spread * noise
        out[name] = jnp.asarray(drawn.astype(out[name].dtype))
    for name, factor in factors.items():
        out[name] = (out[name] * factor).astype(out[name].dtype)
    return out
```

```python
from contextlib import ExitStack

import numpy as np

import concourse.bass as bass
from concourse import mybir

ALU = mybir.AluOpType
ACT = mybir.ActivationFunctionType
AX_X = mybir.AxisListType.X
F32 = mybir.dt.float32
F16 = mybir.dt.float16
BF16 = mybir.dt.bfloat16

P = 128
B, S, D = 8, 512, 128
H = 16
DH = D // H
F = 512
T = S // P
FT = F // P
QUAD = 4
NQ = H // QUAD
LEAD = 6
PARTS = 3
ROWS = PARTS * PARTS * DH
LN_EPS = 1e-5
Q_EPS = 1e-5
SCALE = float(DH) ** -0.5
STACK_DMAS = 1 + PARTS
STACK_LANDED = 16 * STACK_DMAS

SIDE = {
    (0, 0): ("attn_T",), (0, 1): ("heads_T",), (0, 2): ("q",),
    (1, 0): ("k",),
    (2, 1): ("max_T",), (2, 2): ("ffn1_T",),
    (3, 0): ("ffn1_up", 0), (3, 1): ("ffn1_up", 1), (3, 2): ("ffn1_up", 2),
    (4, 0): ("ffn1_up", 3), (4, 1): ("heads_T",), (4, 2): ("ffn1_down", 0),
    (5, 0): ("ffn1_down", 1), (5, 1): ("ffn1_down", 2), (5, 2): ("ffn1_down", 3),
    (6, 0): ("v",), (6, 1): ("max_T",),
    (7, 0): ("out_T",), (7, 2): ("out",),
    (8, 1): ("heads_T",),
    (9, 2): ("ffn2_T",),
    (10, 1): ("max_T",),
    (11, 0): ("ffn2_up", 0), (11, 1): ("ffn2_up", 1), (11, 2): ("ffn2_up", 2),
    (12, 0): ("ffn2_up", 3), (12, 1): ("heads_T",), (12, 2): ("ffn2_down", 0),
    (13, 0): ("ffn2_down", 1), (13, 1): ("ffn2_down", 2), (13, 2): ("ffn2_down", 3),
    (14, 1): ("max_T",),
}
LN = {
    (0, 0): ("stats", "ffn1"), (1, 1): ("apply", "ffn1"),
    (6, 2): ("stats", "attn"), (9, 0): ("apply", "attn"),
    (8, 0): ("stats", "ffn2"), (9, 1): ("apply", "ffn2"),
}


class Phase:

    def __init__(self, i, core=True, next_max=True, ffn1=True, proj=True, post=True):
        self.i, self.core, self.next_max, self.ffn1, self.proj, self.post = i, core, next_max, ffn1, proj, post

    def batch(self, kind):
        return self.i + {"ffn1": 2, "proj": 1, "post": -1}[kind]

    def side(self, step, slot):
        found = SIDE.get((step, slot))
        if found is None:
            return None
        name, arg = found[0], found[1] if len(found) > 1 else 0
        if name == "max_T":
            quad = self.i * NQ + (step // QUAD + 1)
            on = self.core and (step < H - QUAD or self.next_max)
            return (name, arg, quad) if on else None
        if name == "heads_T":
            quad = self.i * NQ + step // QUAD - 2
            on = self.post if step < 2 * QUAD else self.core
            return (name, (step // QUAD - 2) % NQ, quad) if on else None
        kind = {"ffn1": "ffn1", "ffn2": "post", "out": "post"}.get(name.split("_")[0], "proj")
        on = {"ffn1": self.ffn1, "proj": self.proj, "post": self.post}[kind]
        return (name, arg, self.batch(kind)) if on else None

    def ln(self, step, slot):
        found = LN.get((step, slot))
        if found is None:
            return None
        what, which = found
        kind = {"ffn1": "ffn1", "attn": "ffn1", "ffn2": "post"}[which]
        on = {"ffn1": self.ffn1, "post": self.post}[kind]
        return (what, which, self.batch(kind)) if on else None

    def sides(self):
        found = [self.side(s, c) for s in range(H) for c in range(3)]
        return [x for x in found if x]


PROLOGUE = ([("ffn1_T", 0, 0)] + [("ffn1_up", n, 0) for n in range(FT)] + [("ffn1_down", n, 0) for n in range(T)]
            + [("attn_T", 0, 0), ("k", 0, 0), ("q", 0, 0), ("v", 0, 0)]
            + [("ffn1_T", 0, 1)] + [("ffn1_up", n, 1) for n in range(FT)] + [("ffn1_down", n, 1) for n in range(T)])
FIRST = dict(post=False)
BEFORE_LAST = dict(ffn1=False)
LAST = dict(next_max=False, ffn1=False, proj=False)
DRAIN = dict(core=False, next_max=False, ffn1=False, proj=False)
LOOP = (1, B - 2)


def wait(engine, semaphore, value):
    if not isinstance(value, int) or value > 0:
        engine.wait_ge(semaphore, value)


def phases(loop):
    yield Phase(0, **FIRST)
    with loop(*LOOP) as i:
        yield Phase(i)
    yield Phase(B - 2, **BEFORE_LAST)
    yield Phase(B - 1, **LAST)
    yield Phase(B, **DRAIN)


def macaron_layer(nc, x, wq, bq, wk, bk, wv, bv, wo, bo, w1, b1, w2, b2, ident, rope_cos, rope_sin, out):
    with ExitStack() as ctx:
        def sb(name, shape, dt=F32):
            return ctx.enter_context(nc.sbuf_tensor(name, shape, dt))

        def psum(name, shape, dt=F32):
            return ctx.enter_context(nc.psum_tensor(name, shape, dt))

        def sem(name):
            return ctx.enter_context(nc.semaphore(name))

        resid = sb("resid", [P, B * T, D])
        probs = sb("probs", [P, 2 * QUAD, T, S])
        q_stack = sb("q_stack", [P, H, S], BF16)
        k_stack = sb("k_stack", [P, H, S], BF16)
        v_heads = sb("v_heads", [P, T, H, 32])
        v_next = sb("v_next", [P, T, D])
        hidden = sb("hidden", [P, FT, S])
        w1_raw = sb("w1_raw", [P, F])
        w2_raw = sb("w2_raw", [P, FT, D])
        w1_q = sb("w1_q", [P, F], F16)
        w2_q = sb("w2_q", [P, FT, D])
        w_proj = sb("w_proj", [P, 4, D])
        b1_col = sb("b1_col", [P, FT])
        bqk_col = sb("bqk_col", [P, 2])
        rows = sb("rows", [P, 3, D])
        b2_half = sb("b2_half", [P, 1, D])
        ident_f = sb("ident_f", [P, P])
        ident_b = sb("ident_b", [P, P], BF16)
        ones_f = sb("ones_f", [P, P])
        cos_t = sb("cos_t", [P, S])
        sin_t = sb("sin_t", [P, S])
        abs_sum = sb("abs_sum", [P, 2])
        thr = sb("thr", [P, 3, 2])
        is_low = sb("is_low", [P, F])
        is_high = sb("is_high", [P, F])
        minus_half = sb("minus_half", [P, T])
        normed = {n: sb(f"normed_{n}", [P, T, D]) for n in ("ffn1", "attn", "ffn2")}
        stats = {n: sb(f"stats_{n}", [P, T, 6]) for n in normed}
        mean_var = {n: sb(f"mean_var_{n}", [P, T, 2]) for n in normed}
        var_eps = {n: sb(f"var_eps_{n}", [P, T]) for n in normed}
        rstd = {n: sb(f"rstd_{n}", [P, T]) for n in normed}
        xb = {n: sb(f"xb_{n}", [P, T, D]) for n in ("ffn1", "out", "ffn2")}
        x_hi = sb("x_hi", [P, S], F16)
        x_lo = sb("x_lo", [P, S], F16)
        x_T = sb("x_T", [P, S])
        qk = {n: sb(f"{n}_32", [P, S]) for n in "qk"}
        qk_swap = {n: sb(f"{n}_swap", [P, S]) for n in "qk"}
        qk_parts = {n: sb(f"{n}_parts", [P, PARTS, S], BF16) for n in "qk"}
        rope_a = sb("rope_a", [P, S])
        rope_b = sb("rope_b", [P, S])
        maxima = sb("maxima", [P, QUAD * T])
        max_rest = sb("max_rest", [P, QUAD * T])
        max_rest2 = sb("max_rest2", [P, QUAD * T])
        max_parts = sb("max_parts", [P, PARTS, QUAD * T], BF16)
        max_T = sb("max_T", [PARTS * QUAD * T, P], BF16)
        heads = sb("heads", [P, S])
        sums_inv = sb("sums_inv", [P, T, QUAD])
        attn_out = sb("attn_out", [P, T, H, DH])
        attn_T = sb("attn_T", [P, S])

        scores_T = psum("scores_T", [P, 2, 2, S])
        scores = psum("scores", [P, 2, S])
        heads_acc = psum("heads_acc", [P, S])
        side = psum("side", [P, S])
        side_b = side[:].bitcast(BF16)
        side_tiles = side[:].rearrange("p (t d) -> p t d", t=T)

        scratch = {n: nc.dram_tensor(f"{n}_scratch", [DH, PARTS, H, S], BF16, kind="Internal").ap() for n in "qk"}

        s_x0 = sem("x0_landed")
        s_x = sem("x_landed")
        s_ident = sem("ident_landed")
        s_w1 = sem("w1_landed")
        s_w2 = sem("w2_landed")
        s_const = sem("consts_landed")
        s_minus_half = sem("minus_half_set")
        s_ones = sem("ones_set")
        s_k_fill = sem("k_stack_filled")
        s_v_fill = sem("v_heads_filled_with_constants")
        s_b2 = sem("b2_landed")
        s_b2h = sem("b2_half_ready")
        s_ident_b = sem("ident_b_ready")
        s_abs = sem("abs_sum_ready")
        s_gamma = sem("gamma_in_psum")
        s_thr = sem("thresholds_done")
        s_wq = sem("weights_quantised")
        s_stats = {n: sem(f"stats_done_{n}") for n in normed}
        s_var = {n: sem(f"var_ready_{n}") for n in normed}
        s_vareps = {n: sem(f"var_eps_ready_{n}") for n in normed}
        s_rstd = {n: sem(f"rstd_ready_{n}") for n in normed}
        s_normed = {n: sem(f"normed_{n}_ready") for n in normed}
        s_xb = {n: sem(f"xb_{n}_ready") for n in xb}
        s_T = {n: sem(f"normed_T_{n}_in_psum") for n in normed}
        s_hi = {n: sem(f"x_hi_{n}_ready") for n in ("ffn1", "ffn2")}
        s_lo = {n: sem(f"x_lo_{n}_ready") for n in ("ffn1", "ffn2")}
        s_up = {n: sem(f"up_{n}_in_psum") for n in ("ffn1", "ffn2")}
        s_hid = {n: sem(f"hidden_{n}_ready") for n in ("ffn1", "ffn2")}
        s_down = {n: sem(f"down_{n}_in_psum") for n in ("ffn1", "ffn2")}
        s_x1 = sem("x1_ready")
        s_x2 = sem("x2_ready")
        s_y = sem("y_ready")
        s_xT = sem("x_T_ready")
        s_qk_psum = {n: sem(f"{n}_in_psum") for n in "qk"}
        s_qk = {n: sem(f"{n}_32_ready") for n in "qk"}
        s_swap = {n: sem(f"{n}_swap_landed") for n in "qk"}
        s_rope = {n: sem(f"{n}_rope_steps") for n in "qk"}
        s_scratch = {n: sem(f"{n}_scratch_landed") for n in "qk"}
        s_stack = sem("stack_landed")
        s_v_psum = sem("v_in_psum")
        s_v_next = sem("v_next_ready")
        s_v_heads = sem("v_heads_filled")
        s_scores = sem("scores_in_psum")
        s_max = sem("maxima_done")
        s_split = sem("max_split_steps")
        s_maxT_psum = sem("max_T_in_psum")
        s_maxT = sem("max_T_ready")
        s_maxrow = sem("max_rows_landed")
        s_scoresT = sem("scores_T_in_psum")
        s_exp = sem("probs_ready")
        s_pv = sem("heads_acc_done")
        s_heads = sem("heads_ready")
        s_headsT = sem("heads_T_in_psum")
        s_inv = sem("sums_inv_ready")
        s_attn = sem("attn_out_ready")
        s_outT_psum = sem("attn_T_in_psum")
        s_outT = sem("attn_T_ready")
        s_out_psum = sem("out_in_psum")
        s_stored = sem("y_stored")

        s_gate = {n: sem(f"gate_{n}") for n in ("sp", "pe", "dve", "pool")}

        def alone(engine, name, semaphore, value):
            if not isinstance(value, int) or value > 0:
                engine.wait_ge(semaphore, value)
                if not isinstance(value, int):
                    engine.sem_inc(s_gate[name])

        CONST_DMAS = 11
        SPLIT_STEPS = 5
        ROPE_STEPS = 7

        def side_read(name, arg, index):
            if name == "max_T":
                return s_maxT, index + 1
            if name == "heads_T":
                return s_attn, index + 1
            if name in ("q", "k"):
                return s_qk[name], index + 1
            if name in ("ffn1_up", "ffn2_up"):
                return s_hid[name[:4]], index * FT + (arg + 1)
            if name in ("ffn1_T", "ffn2_T"):
                return s_lo[name[:4]], index + 1
            return {"attn_T": s_xT, "v": s_v_next, "out_T": s_outT, "out": s_x2,
                    "ffn1_down": s_x1, "ffn2_down": s_y}[name], index + 1

        block = ctx.enter_context(nc.Block())

        def batch_rows(j):
            return resid[:, bass.ds(j * T, T), :]

        def tile_rows(j, t):
            return resid[:, bass.ds(j * T + t, 1), :].rearrange("p o d -> p (o d)")

        @block.sync
        def _(sp):
            sp.dma_start(resid[:, 0:T, :], x[0].rearrange("(p t) d -> p t d", t=T)).then_inc(s_x0, 16)
            sp.dma_start(w1_raw[:], w1).then_inc(s_w1, 16)
            sp.dma_start(w2_raw[:], w2.rearrange("(n p) d -> p n d", p=P)).then_inc(s_w2, 16)
            sp.dma_start(ident_f[:], ident).then_inc(s_ident, 16)
            sp.dma_start(rows[:, 2, :], b2.partition_broadcast(P)).then_inc(s_b2, 16)
            for n, w in enumerate((wq, wk, wv, wo)):
                sp.dma_start(w_proj[:, n, :], w).then_inc(s_const, 16)
            sp.dma_start(b1_col[:], b1).then_inc(s_const, 16)
            for n, b in enumerate((bq, bk)):
                sp.dma_start(bqk_col[:, n:n + 1], b).then_inc(s_const, 16)
            for n, b in enumerate((bv, bo)):
                sp.dma_start(rows[:, n, :], b.partition_broadcast(P)).then_inc(s_const, 16)
            sp.dma_start(cos_t[:], rope_cos).then_inc(s_const, 16)
            sp.dma_start(sin_t[:], rope_sin).then_inc(s_const, 16)
            for j in range(1, B):
                sp.dma_start(resid[:, j * T:(j + 1) * T, :], x[j].rearrange("(p t) d -> p t d", t=T)).then_inc(s_x, 16)

            def swap(n, j):
                sp.wait_ge(s_qk[n], j + 1)
                sp.dma_start(qk_swap[n][0:P:2, :], qk[n][1:P:2, :]).then_inc(s_swap[n], 16)
                sp.dma_start(qk_swap[n][1:P:2, :], qk[n][0:P:2, :]).then_inc(s_swap[n], 16)

            def to_scratch(n, j):
                alone(sp, "sp", s_rope[n], (j + 1) * ROPE_STEPS)
                wait(sp, s_stack, j * (NQ * STACK_LANDED))
                sp.dma_start(scratch[n].rearrange("d c h t -> h d c t"), qk_parts[n][:]).then_inc(s_scratch[n], 16)

            def stack(j, g):
                hs = slice(g * QUAD, (g + 1) * QUAD)
                alone(sp, "sp", s_scratch["k"], (j + 1) * 16)
                alone(sp, "sp", s_scratch["q"], (j + 1) * 16)
                alone(sp, "sp", s_scoresT, j * (2 * H) + 2 * (QUAD * (g + 1) - H))
                wait(sp, s_stack, (j * NQ + g) * STACK_LANDED)
                src = scratch["q"][:, :, hs, :].rearrange("d c h t -> (d c) (h t)")
                src = bass.AP(src.tensor, src.offset, [[0, PARTS]] + [list(y) for y in src.ap])
                sp.dma_start(q_stack[0:ROWS, hs, :].rearrange("p h t -> p (h t)"), src).then_inc(s_stack, 16)
                for a in range(PARTS):
                    src = scratch["k"][:, a, hs, :].rearrange("d h t -> d (h t)")
                    src = bass.AP(src.tensor, src.offset, [list(src.ap[0]), [0, PARTS], list(src.ap[1])])
                    rows_a = slice(a * DH * PARTS, (a + 1) * DH * PARTS)
                    sp.dma_start(k_stack[rows_a, hs, :].rearrange("p h t -> p (h t)"), src).then_inc(s_stack, 16)

            def max_row(i, g):
                alone(sp, "sp", s_maxT, i * NQ + (g + 1))
                wait(sp, s_maxrow, (i * NQ + g) * 16)
                sp.dma_start(q_stack[ROWS:ROWS + PARTS, g * QUAD:(g + 1) * QUAD, :], max_T[:]).then_inc(s_maxrow, 16)

            sp.wait_ge(s_k_fill, 1)
            swap("k", 0)
            swap("q", 0)
            to_scratch("k", 0)
            to_scratch("q", 0)
            for g in range(NQ):
                stack(0, g)
            max_row(0, 0)
            for ph in phases(sp.Fori):
                i = ph.i
                if ph.proj:
                    swap("k", i + 1)
                    swap("q", i + 1)
                if ph.core:
                    max_row(i, 1)
                    max_row(i, 2)
                if ph.proj:
                    to_scratch("k", i + 1)
                    to_scratch("q", i + 1)
                    stack(i + 1, 0)
                    stack(i + 1, 1)
                if ph.core:
                    max_row(i, 3)
                if ph.proj:
                    stack(i + 1, 2)
                if ph.next_max:
                    max_row(i + 1, 0)
                if ph.post:
                    alone(sp, "sp", s_y, i)
                    sp.dma_start(out[bass.ds(i - 1, 1)].rearrange("b (p t) d -> p (b t) d", t=T),
                                 batch_rows(i - 1)).then_inc(s_stored, 16)
                if ph.proj:
                    stack(i + 1, 3)
            sp.wait_ge(s_stored, 16 * B)

        @block.tensor
        def _(pe):
            def scores_of(i, s, tiles):
                if s % QUAD == 0 and tiles[0] == 0:
                    pe.wait_ge(s_stack, (i * NQ + (s // QUAD + 1)) * STACK_LANDED)
                for t in tiles:
                    wait(pe, s_max, (i * H + s) * T + (t - 1))
                    pe.matmul(scores[:, t % 2, :], q_stack[0:ROWS, s, t * P:(t + 1) * P], k_stack[0:ROWS, s, :],
                              start=True, stop=True).then_inc(s_scores, 1)

            def scores_T_of(i, s, half):
                if s % QUAD == 0 and half == 0:
                    pe.wait_ge(s_maxrow, (i * NQ + (s // QUAD + 1)) * 16)
                wait(pe, s_exp, (i * H + s) * 2 + (half - 1))
                for t in range(2):
                    kt = (2 * half + t) * P
                    mm = pe.matmul(scores_T[:, half, t, :], k_stack[0:ROWS + PARTS, s, kt:kt + P],
                                   q_stack[0:ROWS + PARTS, s, :], start=True, stop=True)
                mm.then_inc(s_scoresT, 1)

            def values(quad, g, kt):
                if kt == 0:
                    pe.wait_ge(s_exp, (quad + 1) * (2 * QUAD))
                    pe.wait_ge(s_v_heads, quad + 1)
                    wait(pe, s_heads, quad)
                for j in range(QUAD):
                    mm = pe.matmul(heads_acc[32 * j:32 * j + 32, :], v_heads[:, kt, g * QUAD + j, :],
                                   probs[:, (g % 2) * QUAD + j, kt, :], start=(kt == 0), stop=(kt == T - 1))
                if kt == T - 1:
                    mm.then_inc(s_pv, 1)

            last = [None]

            def side_work(use):
                if use is None:
                    return
                name, arg, index = use
                if last[0] is not None and not (name.endswith("_down") and arg):
                    pe.wait_ge(*side_read(*last[0]))
                last[0] = use
                which = name.split("_")[0]
                if name == "max_T":
                    alone(pe, "pe", s_split, (index + 1) * SPLIT_STEPS)
                    pe.transpose(side_b[0:PARTS * QUAD * T, 0:P], max_parts[:].rearrange("p c n -> p (c n)"),
                                 ident_b[:]).then_inc(s_maxT_psum, 1)
                elif name == "heads_T":
                    pe.wait_ge(s_heads, index + 1)
                    for t in range(T):
                        mm = pe.transpose(side[:, t * P:(t + 1) * P], heads[:, t * P:(t + 1) * P], ident_f[:])
                    mm.then_inc(s_headsT, 1)
                elif name == "out_T":
                    pe.wait_ge(s_attn, (index + 1) * NQ)
                    for t in range(T):
                        mm = pe.transpose(side[:, t * P:(t + 1) * P],
                                          attn_out[:, t, :, :].rearrange("p h d -> p (h d)"), ident_f[:])
                    mm.then_inc(s_outT_psum, 1)
                elif name in ("ffn1_T", "attn_T", "ffn2_T"):
                    pe.wait_ge(s_normed[which], (index + 1) * T)
                    for t in range(T):
                        mm = pe.transpose(side[:, t * P:(t + 1) * P], normed[which][:, t, :], ident_f[:])
                    mm.then_inc(s_T[which], 1)
                elif name in ("q", "k"):
                    pe.wait_ge(s_xT, index + 1)
                    pe.matmul(side[:], w_proj[:, "qk".index(name), :], x_T[:], start=True,
                              stop=True).then_inc(s_qk_psum[name], 1)
                elif name in ("v", "out"):
                    lhs, w = (x_T, 2) if name == "v" else (attn_T, 3)
                    pe.wait_ge(s_xT if name == "v" else s_outT, index + 1)
                    for t in range(T):
                        mm = pe.matmul(side[:, t * P:(t + 1) * P], lhs[:, t * P:(t + 1) * P], w_proj[:, w, :],
                                       start=True, stop=True)
                    mm.then_inc(s_v_psum if name == "v" else s_out_psum, 1)
                elif name.endswith("_up"):
                    pe.wait_ge(s_lo[which], index + 1)
                    for n, part in enumerate((x_hi, x_lo)):
                        mm = pe.matmul(side[:], w1_q[:, arg * P:(arg + 1) * P], part[:], start=(n == 0), stop=(n == 1))
                    mm.then_inc(s_up[which], 1)
                elif name.endswith("_down"):
                    if arg == 0:
                        pe.wait_ge(s_hid[which], (index + 1) * FT)
                    for n in range(FT):
                        mm = pe.matmul(side[:, arg * P:(arg + 1) * P], hidden[:, n, arg * P:(arg + 1) * P],
                                       w2_q[:, n, :], start=(n == 0), stop=(n == FT - 1))
                    if arg == T - 1:
                        mm.then_inc(s_down[which], 1)

            pe.wait_ge(s_abs, 2)
            pe.wait_ge(s_ones, 1)
            pe.matmul(side[:, 0:2], ones_f[:], abs_sum[:], start=True, stop=True).then_inc(s_gamma, 1)
            pe.wait_ge(s_thr, 1)
            pe.wait_ge(s_wq, 2)
            pe.wait_ge(s_ident_b, 1)
            pe.wait_ge(s_ident, 16)
            pe.wait_ge(s_const, 16 * CONST_DMAS)
            for use in PROLOGUE:
                side_work(use)
            for s in range(LEAD):
                scores_of(0, s, (0, 1, 2, 3))
                if s == QUAD:
                    side_work(("max_T", 0, 0))
            for ph in phases(pe.Fori):
                i = ph.i
                if not isinstance(i, int) or i > 0:
                    last[0] = Phase(i - 1, **(LAST if ph.i is B else {})).sides()[-1]
                for s in range(H):
                    ahead = ph.core and (s < H - LEAD or ph.next_max)
                    ia, sa = (i, s + LEAD) if s < H - LEAD else (i + 1, s + LEAD - H)
                    if ph.core:
                        scores_T_of(i, s, 0)
                    if ahead:
                        scores_of(ia, sa, (0, 1))
                    side_work(ph.side(s, 0))
                    if ph.core:
                        scores_T_of(i, s, 1)
                    if ahead:
                        scores_of(ia, sa, (2, 3))
                    side_work(ph.side(s, 1))
                    if ph.post if s < QUAD else ph.core:
                        values(i * NQ + (s // QUAD - 1), (s // QUAD - 1) % NQ, s % QUAD)
                    side_work(ph.side(s, 2))

        @block.scalar
        def _(act):
            def side_part(use):
                if use is None:
                    return
                name, arg, index = use
                which = name.split("_")[0]
                if name == "max_T":
                    act.wait_ge(s_maxT_psum, index + 1)
                    wait(act, s_maxrow, index * 16)
                    act.activation(max_T[:], side_b[0:PARTS * QUAD * T, 0:P], ACT.Copy).then_inc(s_maxT, 1)
                elif name == "attn_T":
                    act.wait_ge(s_T["attn"], index + 1)
                    act.activation(x_T[:], side[:], ACT.Copy).then_inc(s_xT, 1)
                elif name in ("ffn1_T", "ffn2_T"):
                    act.wait_ge(s_T[which], index + 1)
                    act.activation(x_hi[:], side[:], ACT.Copy).then_inc(s_hi[which], 1)
                elif name in ("q", "k"):
                    act.wait_ge(s_qk_psum[name], index + 1)
                    wait(act, s_rope[name], index * ROPE_STEPS)
                    n = "qk".index(name)
                    act.activation(qk[name][:], side[:], ACT.Identity, bias=bqk_col[:, n:n + 1]).then_inc(s_qk[name], 1)
                elif name.endswith("_up"):
                    act.wait_ge(s_up[which], index * FT + (arg + 1))
                    act.activation(hidden[:, arg, :], side[:], ACT.Relu, bias=b1_col[:, arg:arg + 1]).then_inc(s_hid[which], 1)
                elif name == "out_T":
                    act.wait_ge(s_outT_psum, index + 1)
                    act.activation(attn_T[:], side[:], ACT.Copy).then_inc(s_outT, 1)

            def exps(i, s, half):
                if s % QUAD == 0 and half == 0:
                    wait(act, s_pv, i * NQ + (s // QUAD - 1))
                act.wait_ge(s_scoresT, (i * H + s) * 2 + (half + 1))
                act.activation(probs[:, s % (2 * QUAD), 2 * half:2 * half + 2, :], scores_T[:, half, :, :], ACT.Exp,
                               scale=SCALE).then_inc(s_exp, 1)

            def take_heads(quad):
                act.wait_ge(s_pv, quad + 1)
                wait(act, s_headsT, quad)
                act.activation(heads[:], heads_acc[:], ACT.Copy).then_inc(s_heads, 1)

            act.wait_ge(s_w1, 16)
            act.activation(hidden[:, 0, :], w1_raw[:], ACT.Abs, accum_out=abs_sum[:, 0:1]).then_inc(s_abs, 1)
            act.wait_ge(s_w2, 16)
            act.activation(hidden[:, 1, :], w2_raw[:].rearrange("p n d -> p (n d)"), ACT.Abs,
                           accum_out=abs_sum[:, 1:2]).then_inc(s_abs, 1)
            act.wait_ge(s_const, 16 * CONST_DMAS)
            for use in PROLOGUE:
                side_part(use)
            side_part(("max_T", 0, 0))
            for ph in phases(act.Fori):
                i = ph.i
                for s in range(H):
                    if ph.core:
                        exps(i, s, 0)
                    if s % QUAD == 0 and (ph.post if s < 2 * QUAD else ph.core):
                        take_heads(i * NQ + (s // QUAD - 2))
                    side_part(ph.side(s, 0))
                    if ph.core:
                        exps(i, s, 1)
                    side_part(ph.side(s, 1))
                    side_part(ph.side(s, 2))

        @block.vector
        def _(dve):
            def ln_stats(n, j):
                if n == "ffn1":
                    dve.wait_ge(*((s_x0, 16) if isinstance(j, int) and j == 0 else (s_x, 16 * (B - 1))))
                else:
                    alone(dve, "dve", s_x1 if n == "attn" else s_x2, j + 1)
                for t in range(T):
                    dve.bn_stats(stats[n][:, t, :], tile_rows(j, t)).then_inc(s_stats[n], 1)
                alone(dve, "dve", s_stats[n], (j + 1) * T)
                for t in range(T):
                    dve.bn_aggr(mean_var[n][:, t, :], stats[n][:, t, :]).then_inc(s_var[n], 1)

            def ln_apply(n, j):
                dve.wait_ge(s_rstd[n], j + 1)
                dve.wait_ge(s_var[n], (j + 1) * T)
                wait(dve, s_T[n], j)
                for t in range(T):
                    dve.tensor_scalar(normed[n][:, t, :], tile_rows(j, t), mean_var[n][:, t, 0:1],
                                      rstd[n][:, t:t + 1], ALU.subtract, ALU.mult).then_inc(s_normed[n], 1)

            def norm(use):
                if use is not None:
                    what, n, j = use
                    (ln_stats if what == "stats" else ln_apply)(n, j)

            def max_of(i, s, tiles):
                for t in tiles:
                    dve.wait_ge(s_scores, (i * H + s) * T + (t + 1))
                    if s % QUAD == 0 and t == 0:
                        wait(dve, s_split, (i * NQ + s // QUAD) * SPLIT_STEPS)
                    c = (s % QUAD) * T + t
                    dve.tensor_reduce(maxima[:, c:c + 1], scores[:, t % 2, :], AX_X, ALU.max).then_inc(s_max, 1)

            def split_max(quad):
                n = quad * SPLIT_STEPS
                dve.wait_ge(s_max, (quad + 1) * (QUAD * T))
                wait(dve, s_maxT_psum, quad)
                dve.tensor_copy(max_parts[:, 0, :], maxima[:]).then_inc(s_split, 1)
                dve.wait_ge(s_split, n + 1)
                dve.tensor_tensor(max_rest[:], maxima[:], max_parts[:, 0, :], ALU.subtract).then_inc(s_split, 1)
                dve.wait_ge(s_split, n + 2)
                dve.tensor_copy(max_parts[:, 1, :], max_rest[:]).then_inc(s_split, 1)
                dve.wait_ge(s_split, n + 3)
                dve.tensor_tensor(max_rest2[:], max_rest[:], max_parts[:, 1, :], ALU.subtract).then_inc(s_split, 1)
                dve.wait_ge(s_split, n + 4)
                dve.tensor_copy(max_parts[:, 2, :], max_rest2[:]).then_inc(s_split, 1)

            def side_part(use):
                if use is None:
                    return
                name, arg, index = use
                which = name.split("_")[0]
                if name == "heads_T":
                    per_head = side[:].rearrange("p (t j c) -> p t j c", t=T, j=QUAD)
                    g = arg
                    dve.wait_ge(s_headsT, index + 1)
                    dve.reciprocal(sums_inv[:], per_head[:, :, :, DH]).then_inc(s_inv, 1)
                    dve.wait_ge(s_inv, index + 1)
                    dve.tensor_tensor(attn_out[:, :, g * QUAD:(g + 1) * QUAD, :], per_head[:, :, :, 0:DH],
                                      sums_inv[:].unsqueeze(3).to_broadcast([P, T, QUAD, DH]),
                                      ALU.mult).then_inc(s_attn, 1)
                elif name in ("ffn1_T", "ffn2_T"):
                    dve.wait_ge(s_hi[which], index + 1)
                    dve.tensor_tensor(x_lo[:], side[:], x_hi[:], ALU.subtract).then_inc(s_lo[which], 1)
                elif name == "v":
                    dve.wait_ge(s_v_psum, index + 1)
                    wait(dve, s_v_heads, index * NQ)
                    dve.tensor_tensor(v_next[:], side_tiles, rows[:, 0:1, :].to_broadcast([P, T, D]),
                                      ALU.add).then_inc(s_v_next, 1)
                elif name == "out":
                    dve.wait_ge(s_out_psum, index + 1)
                    dve.wait_ge(s_xb["out"], index + 1)
                    dve.tensor_tensor(batch_rows(index), side_tiles, xb["out"][:], ALU.add).then_inc(s_x2, 1)
                elif name.endswith("_down") and arg == T - 1:
                    dve.wait_ge(s_down[which], index + 1)
                    dve.wait_ge(s_xb[which], index + 1)
                    dve.tensor_tensor(batch_rows(index), side_tiles, xb[which][:], ALU.add)\
                       .then_inc(s_x1 if which == "ffn1" else s_y, 1)

            dve.memset(ones_f[:], 1.0).then_inc(s_ones, 1)
            dve.memset(minus_half[:], -0.5).then_inc(s_minus_half, 1)
            norm(("stats", "ffn1", 0))
            dve.memset(k_stack[64:96, :, :], -1.0).then_inc(s_k_fill, 1)
            dve.wait_ge(s_ident, 16)
            dve.tensor_copy(ident_b[:], ident_f[:]).then_inc(s_ident_b, 1)
            dve.wait_ge(s_b2, 16)
            dve.tensor_scalar(b2_half[:], rows[:, 2:3, :], 0.5, None, ALU.mult).then_inc(s_b2h, 1)
            norm(("apply", "ffn1", 0))
            dve.wait_ge(s_gamma, 1)
            dve.tensor_scalar(thr[:, 0, :], side[:, 0:2], 1.0 / (F * D), Q_EPS, ALU.mult, ALU.add).then_inc(s_thr, 1)
            dve.wait_ge(s_thr, 1)
            dve.tensor_scalar(thr[:, 1, :], thr[:, 0, :], 0.5, None, ALU.mult).then_inc(s_thr, 1)
            dve.tensor_scalar(thr[:, 2, :], thr[:, 0, :], -0.5, None, ALU.mult).then_inc(s_thr, 1)
            dve.wait_ge(s_thr, 3)
            dve.tensor_scalar(is_low[:], w1_raw[:], thr[:, 2, 0:1], None, ALU.is_lt).then_inc(s_thr, 1)
            dve.wait_ge(s_thr, 4)
            dve.scalar_tensor_tensor(out=w1_q[:], in0=w1_raw[:], scalar=thr[:, 1, 0:1], in1=is_low[:],
                                     op0=ALU.is_gt, op1=ALU.subtract).then_inc(s_wq, 1)
            dve.wait_ge(s_wq, 1)
            w2_flat = w2_raw[:].rearrange("p n d -> p (n d)")
            dve.tensor_scalar(is_low[:], w2_flat, thr[:, 2, 1:2], 0.5, ALU.is_lt, ALU.mult).then_inc(s_thr, 1)
            dve.tensor_scalar(is_high[:], w2_flat, thr[:, 1, 1:2], 0.5, ALU.is_gt, ALU.mult).then_inc(s_thr, 1)
            dve.wait_ge(s_thr, 6)
            dve.tensor_tensor(w2_q[:].rearrange("p n d -> p (n d)"), is_high[:], is_low[:], ALU.subtract).then_inc(s_wq, 1)
            dve.wait_ge(s_const, 16 * CONST_DMAS)
            dve.memset(v_heads[:], 0.0).then_inc(s_v_fill, 1)
            dve.wait_ge(s_v_fill, 1)
            dve.memset(v_heads[:, :, :, DH], 1.0).then_inc(s_v_fill, 1)
            for use in PROLOGUE:
                side_part(use)
                if use[0] == "ffn1_down" and use[1] == T - 1:
                    norm(("stats", "attn", use[2]))
                    norm(("apply", "attn", use[2]))
                    if use[2] == 0:
                        norm(("stats", "ffn1", 1))
                        norm(("apply", "ffn1", 1))
            for s in range(LEAD):
                max_of(0, s, (0, 1, 2, 3))
                if s == QUAD - 1:
                    split_max(0)
            for ph in phases(dve.Fori):
                i = ph.i
                for s in range(H):
                    ahead = ph.core and (s < H - LEAD or ph.next_max)
                    ia, sa = (i, s + LEAD) if s < H - LEAD else (i + 1, s + LEAD - H)
                    if ahead:
                        max_of(ia, sa, (0, 1))
                    side_part(ph.side(s, 0))
                    norm(ph.ln(s, 0))
                    if ahead:
                        max_of(ia, sa, (2, 3))
                        if sa % QUAD == QUAD - 1:
                            split_max(ia * NQ + sa // QUAD)
                    side_part(ph.side(s, 1))
                    norm(ph.ln(s, 1))
                    side_part(ph.side(s, 2))
                    norm(ph.ln(s, 2))

        @block.gpsimd
        def _(pool):
            def inv_std(n, j):
                pool.wait_ge(s_var[n], (j + 1) * T)
                alone(pool, "pool", s_normed[n], j * T)
                pool.tensor_scalar(var_eps[n][:], mean_var[n][:, :, 1], LN_EPS, None, ALU.add).then_inc(s_vareps[n], 1)
                pool.wait_ge(s_vareps[n], j + 1)
                pool.tensor_tensor(rstd[n][:], var_eps[n][:], minus_half[:], ALU.pow).then_inc(s_rstd[n], 1)

            def add_bias(n, j):
                ready, used, bias = {"ffn1": (None, s_x1, b2_half[:]), "out": (s_x1, s_x2, rows[:, 1:2, :]),
                                     "ffn2": (s_x2, s_y, b2_half[:])}[n]
                if ready is None:
                    pool.wait_ge(*((s_x0, 16) if isinstance(j, int) and j == 0 else (s_x, 16 * (B - 1))))
                else:
                    pool.wait_ge(ready, j + 1)
                alone(pool, "pool", used, j)
                pool.tensor_tensor(xb[n][:], batch_rows(j), bias.to_broadcast([P, T, D]), ALU.add).then_inc(s_xb[n], 1)

            def rotate(n, j):
                done = j * ROPE_STEPS
                pool.wait_ge(s_qk[n], j + 1)
                other, count = ("q", done) if n == "k" else ("k", done + ROPE_STEPS)
                wait(pool, s_rope[other], count)
                pool.tensor_tensor(rope_a[:], qk[n][:], cos_t[:], ALU.mult).then_inc(s_rope[n], 1)
                pool.wait_ge(s_swap[n], (j + 1) * 32)
                pool.tensor_tensor(rope_b[:], qk_swap[n][:], sin_t[:], ALU.mult).then_inc(s_rope[n], 1)
                pool.wait_ge(s_rope[n], done + 2)
                pool.tensor_tensor(rope_a[:], rope_a[:], rope_b[:], ALU.add).then_inc(s_rope[n], 1)
                pool.wait_ge(s_rope[n], done + 3)
                alone(pool, "pool", s_scratch[n], j * 16)
                pool.tensor_scalar(qk_parts[n][:, 0, :], rope_a[:], 1.0, 0.0, ALU.mult, ALU.add).then_inc(s_rope[n], 1)
                pool.wait_ge(s_rope[n], done + 4)
                pool.tensor_tensor(rope_b[:], rope_a[:], qk_parts[n][:, 0, :], ALU.subtract).then_inc(s_rope[n], 1)
                alone(pool, "pool", s_rope[n], done + 5)
                pool.tensor_scalar(qk_parts[n][:, 1, :], rope_b[:], 1.0, 0.0, ALU.mult, ALU.add).then_inc(s_rope[n], 1)
                pool.wait_ge(s_rope[n], done + 6)
                pool.tensor_tensor(qk_parts[n][:, 2, :], rope_b[:], qk_parts[n][:, 1, :], ALU.subtract).then_inc(s_rope[n], 1)

            def fill_values(j, g):
                pool.wait_ge(s_v_next, j + 1)
                alone(pool, "pool", s_pv, j * NQ + (g + 1 - NQ))
                pool.tensor_scalar(v_heads[:, :, g * QUAD:(g + 1) * QUAD, 0:DH],
                                   v_next[:].rearrange("p t (h c) -> p t h c", h=H)[:, :, g * QUAD:(g + 1) * QUAD, :],
                                   1.0, 0.0, ALU.mult, ALU.add).then_inc(s_v_heads, 1)

            pool.wait_ge(s_minus_half, 1)
            inv_std("ffn1", 0)
            pool.wait_ge(s_b2h, 1)
            add_bias("ffn1", 0)
            inv_std("attn", 0)
            inv_std("ffn1", 1)
            add_bias("ffn1", 1)
            pool.wait_ge(s_const, 16 * CONST_DMAS)
            rotate("k", 0)
            rotate("q", 0)
            pool.wait_ge(s_v_fill, 2)
            fill_values(0, 0)
            fill_values(0, 1)
            inv_std("attn", 1)
            for ph in phases(pool.Fori):
                i = ph.i
                if ph.core:
                    fill_values(i, 2)
                if ph.ffn1:
                    inv_std("ffn1", i + 2)
                    add_bias("ffn1", i + 2)
                if ph.proj:
                    rotate("k", i + 1)
                if ph.core:
                    fill_values(i, 3)
                if ph.post:
                    add_bias("out", i - 1)
                if ph.proj:
                    rotate("q", i + 1)
                if ph.ffn1:
                    inv_std("attn", i + 2)
                if ph.post:
                    inv_std("ffn2", i - 1)
                    add_bias("ffn2", i - 1)
                if ph.proj:
                    fill_values(i + 1, 0)
                    fill_values(i + 1, 1)


def kernel(**inputs):
    import concourse.bacc as bacc
    from concourse.bass_utils import run_bass_kernel_spmd

    def given(name, transpose=False):
        a = np.asarray(inputs[name])
        return np.ascontiguousarray(a.T if transpose else a)

    position = (np.arange(P)[None, :] * T + np.arange(T)[:, None]).reshape(-1).astype(np.float32)
    channel = np.arange(D) % DH
    inv_freq = (1.0 / np.float32(10000.0) ** (np.arange(0, DH, 2, dtype=np.float32) / np.float32(DH))).astype(np.float32)
    theta = (position[None, :] * inv_freq[channel // 2][:, None]).astype(np.float32)
    sign = np.where(channel % 2 == 0, -1.0, 1.0).astype(np.float32)[:, None]
    arrays = {
        "x": given("L0_attn_x"),
        "wq": given("L0_attn_Wq", True), "bq": given("L0_attn_bq").reshape(D, 1),
        "wk": given("L0_attn_Wk", True), "bk": given("L0_attn_bk").reshape(D, 1),
        "wv": given("L0_attn_Wv", True), "bv": given("L0_attn_bv"),
        "wo": given("L0_attn_Wo", True), "bo": given("L0_attn_bo"),
        "w1": given("L0_ffn_W1", True), "b1": np.ascontiguousarray(given("L0_ffn_b1").reshape(FT, P).T),
        "w2": given("L0_ffn_W2", True), "b2": given("L0_ffn_b2"),
        "ident": np.eye(P, dtype=np.float32),
        "rope_cos": np.cos(theta), "rope_sin": sign * np.sin(theta),
    }
    nc = bacc.Bacc("TRN2", target_bir_lowering=False, num_devices=1)
    args = [nc.dram_tensor(f"in_{n}", a.shape, mybir.dt.from_np(a.dtype), kind="ExternalInput").ap()
            for n, a in arrays.items()]
    out = nc.dram_tensor("out_y", (B, S, D), F32, kind="ExternalOutput").ap()
    macaron_layer(nc, *args, out)
    r = run_bass_kernel_spmd(nc, [{f"in_{n}": a for n, a in arrays.items()}], core_ids=[0])
    return r.results[0]["out_y"]
```

```python
from contextlib import ExitStack

import numpy as np

import concourse.bass as bass
from concourse import mybir

ALU = mybir.AluOpType
ACT = mybir.ActivationFunctionType
AX_X = mybir.AxisListType.X
F32 = mybir.dt.float32
F16 = mybir.dt.float16
BF16 = mybir.dt.bfloat16

P = 128
B, S, D = 8, 512, 128
H = 16
DH = D // H
F = 512
T = S // P
FT = F // P
NST = 2
NSC = 3
QUAD = 4
NQ = H // QUAD
LEAD = 7
PARTS = 3
ROWS = PARTS * PARTS * DH
LN_EPS = 1e-5
Q_EPS = 1e-5
SCALE = float(DH) ** -0.5
STACK_DMAS = 1 + PARTS
STACK_LANDED = 16 * STACK_DMAS

SIDE = {
    (0, 0): ("attn_T", 0, 0), (0, 2): ("heads_T", 0, 1),
    (1, 0): ("k", 0, 0), (1, 2): ("max_T", 0, 1),
    (2, 1): ("ffn1_T", 0, 1), (2, 2): ("q", 0, 0),
    (3, 1): ("ffn1_up", 0, 1), (3, 2): ("ffn1_up", 1, 0),
    (4, 0): ("ffn1_up", 2, 1), (4, 1): ("ffn1_up", 3, 0), (4, 2): ("heads_T", 0, 1),
    (5, 0): ("ffn1_down", 0, 0), (5, 1): ("out_T", 0, 1), (5, 2): ("max_T", 0, 1),
    (6, 0): ("ffn1_down", 1, 0), (6, 1): ("out", 0, 1),
    (7, 0): ("ffn1_down", 2, 0), (7, 1): ("ffn1_down", 3, 0),
    (8, 1): ("ffn2_T", 0, 1),
    (9, 0): ("heads_T", 0, 1), (9, 1): ("ffn2_up", 0, 0), (9, 2): ("max_T", 0, 1),
    (10, 0): ("ffn2_up", 1, 0), (10, 1): ("ffn2_up", 2, 1), (10, 2): ("ffn2_up", 3, 0),
    (11, 1): ("ffn2_down", 0, 0),
    (12, 0): ("ffn2_down", 1, 0), (12, 2): ("heads_T", 0, 1),
    (13, 0): ("ffn2_down", 2, 0), (13, 1): ("max_T", 0, 1),
    (14, 0): ("ffn2_down", 3, 0),
    (15, 1): ("v", 0, 0),
}
LN = {(0, 1): ("stats", "ffn1"), (1, 2): ("apply_first", "ffn1"), (2, 0): ("apply_rest", "ffn1"),
    (6, 1): ("stats", "ffn2"), (7, 2): ("apply_first", "ffn2"), (8, 0): ("apply_rest", "ffn2"),
    (11, 0): ("stats", "attn"), (14, 0): ("apply_first", "attn"), (14, 1): ("apply_rest", "attn"),
}


class Phase:

    def __init__(self, i, core=True, next_max=True, ffn1=True, proj=True, post=True):
        self.i, self.core, self.next_max, self.ffn1, self.proj, self.post = i, core, next_max, ffn1, proj, post

    def batch(self, kind):
        return self.i + {"ffn1": 2, "proj": 1, "post": -1}[kind]

    def side(self, step, slot):
        found = SIDE.get((step, slot))
        if found is None:
            return None
        name, arg, bank = found
        if name == "max_T":
            quad = self.i * NQ + (step // QUAD + 1)
            on = self.core and (step < H - QUAD or self.next_max)
            return (name, arg, quad, bank) if on else None
        if name == "heads_T":
            quad = self.i * NQ + step // QUAD - 2
            on = self.post if step < 2 * QUAD else self.core
            return (name, (step // QUAD - 2) % NQ, quad, bank) if on else None
        kind = {"ffn1": "ffn1", "ffn2": "post", "out": "post"}.get(name.split("_")[0], "proj")
        on = {"ffn1": self.ffn1, "proj": self.proj, "post": self.post}[kind]
        return (name, arg, self.batch(kind), bank) if on else None

    def ln(self, step, slot):
        found = LN.get((step, slot))
        if found is None:
            return None
        what, which = found
        kind = {"ffn1": "ffn1", "attn": "ffn1", "ffn2": "post"}[which]
        on = {"ffn1": self.ffn1, "post": self.post}[kind]
        return (what, which, self.batch(kind)) if on else None

    def last_side(self, bank):
        found = [self.side(s, c) for s in range(H) for c in range(3)]
        return [x for x in found if x and x[3] == bank][-1]


def first_ffn(j):
    return ([("ffn1_T", 0, j, 0)] + [("ffn1_up", n, j, 1 - n % 2) for n in range(FT)]
            + [("ffn1_down", n, j, 1) for n in range(T)])


PROLOGUE = (first_ffn(0) + [("attn_T", 0, 0, 0), ("k", 0, 0, 1), ("q", 0, 0, 0), ("v", 0, 0, 1)] + first_ffn(1))
FIRST = dict(post=False)
BEFORE_LAST = dict(ffn1=False)
LAST = dict(next_max=False, ffn1=False, proj=False)
DRAIN = dict(core=False, next_max=False, ffn1=False, proj=False)
LOOP = (1, B - 2)


def wait(engine, semaphore, value):
    if not isinstance(value, int) or value > 0:
        engine.wait_ge(semaphore, value)


def phases(loop):
    yield Phase(0, **FIRST)
    with loop(*LOOP) as i:
        yield Phase(i)
    yield Phase(B - 2, **BEFORE_LAST)
    yield Phase(B - 1, **LAST)
    yield Phase(B, **DRAIN)


def macaron_layer(nc, x, wq, bq, wk, bk, wv, bv, wo, bo, w1, b1, w2, b2, ident, rope_cos, rope_sin, out):
    with ExitStack() as ctx:
        def sb(name, shape, dt=F32):
            return ctx.enter_context(nc.sbuf_tensor(name, shape, dt))

        def psum(name, shape, dt=F32):
            return ctx.enter_context(nc.psum_tensor(name, shape, dt))

        def sem(name):
            return ctx.enter_context(nc.semaphore(name))

        resid = sb("resid", [P, B * T, D])
        probs = sb("probs", [P, 2 * QUAD, T, S])
        q_stack = sb("q_stack", [P, H, S], BF16)
        k_stack = sb("k_stack", [P, H, S], BF16)
        v_heads = sb("v_heads", [P, T, H, 32])
        v_next = sb("v_next", [P, T, D])
        hidden = sb("hidden", [P, FT, S])
        w1_raw = sb("w1_raw", [P, F])
        w2_raw = sb("w2_raw", [P, FT, D])
        w1_q = sb("w1_q", [P, F], F16)
        w2_q = sb("w2_q", [P, FT, D])
        w_proj = sb("w_proj", [P, 4, D])
        b1_col = sb("b1_col", [P, FT])
        bqk_col = sb("bqk_col", [P, 2])
        rows = sb("rows", [P, 3, D])
        b2_half = sb("b2_half", [P, 1, D])
        ident_f = sb("ident_f", [P, P])
        ident_b = sb("ident_b", [P, P], BF16)
        ones_f = sb("ones_f", [P, P])
        cos_t = sb("cos_t", [P, S])
        sin_t = sb("sin_t", [P, S])
        abs_sum = sb("abs_sum", [P, 2])
        thr = sb("thr", [P, 3, 2])
        is_low = sb("is_low", [P, F])
        is_high = sb("is_high", [P, F])
        minus_half = sb("minus_half", [P, T])
        normed = {n: sb(f"normed_{n}", [P, T, D]) for n in ("ffn1", "attn", "ffn2")}
        stats = {n: sb(f"stats_{n}", [P, T, 6]) for n in normed}
        mean_var = {n: sb(f"mean_var_{n}", [P, T, 2]) for n in normed}
        var_eps = {n: sb(f"var_eps_{n}", [P, T]) for n in normed}
        rstd = {n: sb(f"rstd_{n}", [P, T]) for n in normed}
        xb = {n: sb(f"xb_{n}", [P, T, D]) for n in ("ffn1", "out", "ffn2")}
        x_hi = sb("x_hi", [P, S], F16)
        x_lo = sb("x_lo", [P, S], F16)
        x_T = sb("x_T", [P, S])
        qk = {n: sb(f"{n}_32", [P, S]) for n in "qk"}
        qk_swap = {n: sb(f"{n}_swap", [P, S]) for n in "qk"}
        qk_parts = {n: sb(f"{n}_parts", [P, PARTS, S], BF16) for n in "qk"}
        rope_a = sb("rope_a", [P, S])
        rope_b = sb("rope_b", [P, S])
        maxima = sb("maxima", [P, QUAD * T])
        max_rest = sb("max_rest", [P, QUAD * T])
        max_rest2 = sb("max_rest2", [P, QUAD * T])
        max_parts = sb("max_parts", [P, PARTS, QUAD * T], BF16)
        max_T = sb("max_T", [PARTS * QUAD * T, P], BF16)
        heads = sb("heads", [P, S])
        sums_inv = sb("sums_inv", [P, T, QUAD])
        attn_out = sb("attn_out", [P, T, H, DH])
        attn_T = sb("attn_T", [P, S])

        scores_T = psum("scores_T", [P, NST, S])
        scores = psum("scores", [P, NSC, S])
        heads_acc = psum("heads_acc", [P, S])
        side = psum("side", [P, 2, S])

        scratch = {n: nc.dram_tensor(f"{n}_scratch", [DH, PARTS, H, S], BF16, kind="Internal").ap() for n in "qk"}

        s_x0 = sem("x0_landed")
        s_x = sem("x_landed")
        s_ident = sem("ident_landed")
        s_w1 = sem("w1_landed")
        s_w2 = sem("w2_landed")
        s_const = sem("consts_landed")
        s_minus_half = sem("minus_half_set")
        s_ones = sem("ones_set")
        s_k_fill = sem("k_stack_filled")
        s_v_fill = sem("v_heads_filled_with_constants")
        s_b2 = sem("b2_landed")
        s_b2h = sem("b2_half_ready")
        s_ident_b = sem("ident_b_ready")
        s_abs = sem("abs_sum_ready")
        s_gamma = sem("gamma_in_psum")
        s_thr = sem("thresholds_done")
        s_wq = sem("weights_quantised")
        s_stats = {n: sem(f"stats_done_{n}") for n in normed}
        s_var = {n: sem(f"var_ready_{n}") for n in normed}
        s_vareps = {n: sem(f"var_eps_ready_{n}") for n in normed}
        s_rstd = {n: sem(f"rstd_ready_{n}") for n in normed}
        s_normed = {n: sem(f"normed_{n}_ready") for n in normed}
        s_xb = {n: sem(f"xb_{n}_ready") for n in xb}
        s_T = {n: sem(f"normed_T_{n}_in_psum") for n in normed}
        s_hi = {n: sem(f"x_hi_{n}_ready") for n in ("ffn1", "ffn2")}
        s_lo = {n: sem(f"x_lo_{n}_ready") for n in ("ffn1", "ffn2")}
        s_up = {n: sem(f"up_{n}_in_psum") for n in ("ffn1", "ffn2")}
        s_hid = {n: sem(f"hidden_{n}_ready") for n in ("ffn1", "ffn2")}
        s_down = {n: sem(f"down_{n}_in_psum") for n in ("ffn1", "ffn2")}
        s_x1 = sem("x1_ready")
        s_x2 = sem("x2_ready")
        s_y = sem("y_ready")
        s_xT = sem("x_T_ready")
        s_qk_psum = {n: sem(f"{n}_in_psum") for n in "qk"}
        s_qk = {n: sem(f"{n}_32_ready") for n in "qk"}
        s_swap = {n: sem(f"{n}_swap_landed") for n in "qk"}
        s_rope = {n: sem(f"{n}_rope_steps") for n in "qk"}
        s_scratch = {n: sem(f"{n}_scratch_landed") for n in "qk"}
        s_stack = sem("stack_landed")
        s_v_psum = sem("v_in_psum")
        s_v_next = sem("v_next_ready")
        s_v_heads = sem("v_heads_filled")
        s_scores = sem("scores_in_psum")
        s_max = sem("maxima_done")
        s_split = sem("max_split_steps")
        s_maxT_psum = sem("max_T_in_psum")
        s_maxT = sem("max_T_ready")
        s_maxrow = sem("max_rows_landed")
        s_scoresT = sem("scores_T_in_psum")
        s_exp = sem("probs_ready")
        s_pv = sem("heads_acc_done")
        s_heads = sem("heads_ready")
        s_headsT = sem("heads_T_in_psum")
        s_inv = sem("sums_inv_ready")
        s_attn = sem("attn_out_ready")
        s_outT_psum = sem("attn_T_in_psum")
        s_outT = sem("attn_T_ready")
        s_out_psum = sem("out_in_psum")
        s_stored = sem("y_stored")

        s_gate = {n: sem(f"gate_{n}") for n in ("sp", "pe", "dve", "pool")}

        def alone(engine, name, semaphore, value):
            if not isinstance(value, int) or value > 0:
                engine.wait_ge(semaphore, value)
                if not isinstance(value, int):
                    engine.sem_inc(s_gate[name])

        CONST_DMAS = 11
        SPLIT_STEPS = 5
        ROPE_STEPS = 7

        def side_read(name, arg, index, bank):
            if name == "max_T":
                return s_maxT, index + 1
            if name == "heads_T":
                return s_attn, index + 1
            if name in ("q", "k"):
                return s_qk[name], index + 1
            if name in ("ffn1_up", "ffn2_up"):
                return s_hid[name[:4]], index * FT + (arg + 1)
            if name in ("ffn1_T", "ffn2_T"):
                return s_lo[name[:4]], index + 1
            return {"attn_T": s_xT, "v": s_v_next, "out_T": s_outT, "out": s_x2,
                    "ffn1_down": s_x1, "ffn2_down": s_y}[name], index + 1

        block = ctx.enter_context(nc.Block())

        def bank_of(n, banks):
            return 1 if n == H * T - 1 and (n + 1) % banks == 1 else n % banks

        def bank_used(n, banks):
            last = n - 1
            while bank_of(last % (H * T), banks) != bank_of(n, banks):
                last -= 1
            return last + 1

        def batch_rows(j):
            return resid[:, bass.ds(j * T, T), :]

        def tile_rows(j, t):
            return resid[:, bass.ds(j * T + t, 1), :].rearrange("p o d -> p (o d)")

        @block.sync
        def _(sp):
            sp.dma_start(resid[:, 0:T, :], x[0].rearrange("(p t) d -> p t d", t=T)).then_inc(s_x0, 16)
            sp.dma_start(w1_raw[:], w1).then_inc(s_w1, 16)
            sp.dma_start(w2_raw[:], w2.rearrange("(n p) d -> p n d", p=P)).then_inc(s_w2, 16)
            sp.dma_start(ident_f[:], ident).then_inc(s_ident, 16)
            sp.dma_start(rows[:, 2, :], b2.partition_broadcast(P)).then_inc(s_b2, 16)
            for n, w in enumerate((wq, wk, wv, wo)):
                sp.dma_start(w_proj[:, n, :], w).then_inc(s_const, 16)
            sp.dma_start(b1_col[:], b1).then_inc(s_const, 16)
            for n, b in enumerate((bq, bk)):
                sp.dma_start(bqk_col[:, n:n + 1], b).then_inc(s_const, 16)
            for n, b in enumerate((bv, bo)):
                sp.dma_start(rows[:, n, :], b.partition_broadcast(P)).then_inc(s_const, 16)
            sp.dma_start(cos_t[:], rope_cos).then_inc(s_const, 16)
            sp.dma_start(sin_t[:], rope_sin).then_inc(s_const, 16)
            for j in range(1, B):
                sp.dma_start(resid[:, j * T:(j + 1) * T, :], x[j].rearrange("(p t) d -> p t d", t=T)).then_inc(s_x, 16)

            def swap(n, j):
                sp.wait_ge(s_qk[n], j + 1)
                sp.dma_start(qk_swap[n][0:P:2, :], qk[n][1:P:2, :]).then_inc(s_swap[n], 16)
                sp.dma_start(qk_swap[n][1:P:2, :], qk[n][0:P:2, :]).then_inc(s_swap[n], 16)

            def to_scratch(n, j):
                alone(sp, "sp", s_rope[n], (j + 1) * ROPE_STEPS)
                wait(sp, s_stack, j * (NQ * STACK_LANDED))
                sp.dma_start(scratch[n].rearrange("d c h t -> h d c t"), qk_parts[n][:]).then_inc(s_scratch[n], 16)

            def stack(j, g):
                hs = slice(g * QUAD, (g + 1) * QUAD)
                alone(sp, "sp", s_scratch["k"], (j + 1) * 16)
                alone(sp, "sp", s_scratch["q"], (j + 1) * 16)
                alone(sp, "sp", s_scoresT, j * (H * T) + T * (QUAD * (g + 1) - H))
                wait(sp, s_stack, (j * NQ + g) * STACK_LANDED)
                src = scratch["q"][:, :, hs, :].rearrange("d c h t -> (d c) (h t)")
                src = bass.AP(src.tensor, src.offset, [[0, PARTS]] + [list(y) for y in src.ap])
                sp.dma_start(q_stack[0:ROWS, hs, :].rearrange("p h t -> p (h t)"), src).then_inc(s_stack, 16)
                for a in range(PARTS):
                    src = scratch["k"][:, a, hs, :].rearrange("d h t -> d (h t)")
                    src = bass.AP(src.tensor, src.offset, [list(src.ap[0]), [0, PARTS], list(src.ap[1])])
                    rows_a = slice(a * DH * PARTS, (a + 1) * DH * PARTS)
                    sp.dma_start(k_stack[rows_a, hs, :].rearrange("p h t -> p (h t)"), src).then_inc(s_stack, 16)

            def max_row(i, g):
                alone(sp, "sp", s_maxT, i * NQ + (g + 1))
                wait(sp, s_maxrow, (i * NQ + g) * 16)
                sp.dma_start(q_stack[ROWS:ROWS + PARTS, g * QUAD:(g + 1) * QUAD, :], max_T[:]).then_inc(s_maxrow, 16)

            sp.wait_ge(s_k_fill, 1)
            swap("k", 0)
            swap("q", 0)
            to_scratch("k", 0)
            to_scratch("q", 0)
            for g in range(NQ):
                stack(0, g)
            max_row(0, 0)
            for ph in phases(sp.Fori):
                i = ph.i
                if ph.proj:
                    swap("k", i + 1)
                if ph.core:
                    max_row(i, 1)
                if ph.proj:
                    swap("q", i + 1)
                    to_scratch("k", i + 1)
                    to_scratch("q", i + 1)
                if ph.core:
                    max_row(i, 2)
                if ph.proj:
                    stack(i + 1, 0)
                    stack(i + 1, 1)
                if ph.core:
                    max_row(i, 3)
                if ph.proj:
                    stack(i + 1, 2)
                if ph.next_max:
                    max_row(i + 1, 0)
                if ph.post:
                    alone(sp, "sp", s_y, i)
                    sp.dma_start(out[bass.ds(i - 1, 1)].rearrange("b (p t) d -> p (b t) d", t=T),
                                 batch_rows(i - 1)).then_inc(s_stored, 16)
                if ph.proj:
                    stack(i + 1, 3)
            sp.wait_ge(s_stored, 16 * B)

        @block.tensor
        def _(pe):
            def scores_of(i, s, tiles):
                if s % QUAD == 0 and 0 in tiles:
                    pe.wait_ge(s_stack, (i * NQ + (s // QUAD + 1)) * STACK_LANDED)
                for t in tiles:
                    n = s * T + t
                    wait(pe, s_max, i * (H * T) + bank_used(n, NSC))
                    pe.matmul(scores[:, bank_of(n, NSC), :], q_stack[0:ROWS, s, t * P:(t + 1) * P], k_stack[0:ROWS, s, :],
                              start=True, stop=True).then_inc(s_scores, 1)

            def scores_T_of(i, s, t):
                n = s * T + t
                if s % QUAD == 0 and t == 0:
                    pe.wait_ge(s_maxrow, (i * NQ + (s // QUAD + 1)) * 16)
                wait(pe, s_exp, i * (H * T) + bank_used(n, NST))
                pe.matmul(scores_T[:, bank_of(n, NST), :], k_stack[0:ROWS + PARTS, s, t * P:(t + 1) * P],
                          q_stack[0:ROWS + PARTS, s, :], start=True, stop=True).then_inc(s_scoresT, 1)

            def values(quad, g, kt):
                if kt == 0:
                    pe.wait_ge(s_exp, (quad + 1) * (T * QUAD))
                    pe.wait_ge(s_v_heads, quad + 1)
                    wait(pe, s_heads, quad)
                for j in range(QUAD):
                    mm = pe.matmul(heads_acc[32 * j:32 * j + 32, :], v_heads[:, kt, g * QUAD + j, :],
                                   probs[:, (g % 2) * QUAD + j, kt, :], start=(kt == 0), stop=(kt == T - 1))
                if kt == T - 1:
                    mm.then_inc(s_pv, 1)

            last = [None, None]

            def side_work(use):
                if use is None:
                    return
                name, arg, index, b = use
                if last[b] is not None and not (name.endswith("_down") and arg):
                    pe.wait_ge(*side_read(*last[b]))
                last[b] = use
                which = name.split("_")[0]
                if name == "max_T":
                    alone(pe, "pe", s_split, (index + 1) * SPLIT_STEPS)
                    pe.transpose(side[:, b, :].bitcast(BF16)[0:PARTS * QUAD * T, 0:P], max_parts[:].rearrange("p c n -> p (c n)"),
                                 ident_b[:]).then_inc(s_maxT_psum, 1)
                elif name == "heads_T":
                    pe.wait_ge(s_heads, index + 1)
                    for t in range(T):
                        mm = pe.transpose(side[:, b, t * P:(t + 1) * P], heads[:, t * P:(t + 1) * P], ident_f[:])
                    mm.then_inc(s_headsT, 1)
                elif name == "out_T":
                    pe.wait_ge(s_attn, (index + 1) * NQ)
                    for t in range(T):
                        mm = pe.transpose(side[:, b, t * P:(t + 1) * P],
                                          attn_out[:, t, :, :].rearrange("p h d -> p (h d)"), ident_f[:])
                    mm.then_inc(s_outT_psum, 1)
                elif name in ("ffn1_T", "attn_T", "ffn2_T"):
                    pe.wait_ge(s_normed[which], (index + 1) * T)
                    for t in range(T):
                        mm = pe.transpose(side[:, b, t * P:(t + 1) * P], normed[which][:, t, :], ident_f[:])
                    mm.then_inc(s_T[which], 1)
                elif name in ("q", "k"):
                    pe.wait_ge(s_xT, index + 1)
                    pe.matmul(side[:, b, :], w_proj[:, "qk".index(name), :], x_T[:], start=True,
                              stop=True).then_inc(s_qk_psum[name], 1)
                elif name in ("v", "out"):
                    lhs, w = (x_T, 2) if name == "v" else (attn_T, 3)
                    pe.wait_ge(s_xT if name == "v" else s_outT, index + 1)
                    for t in range(T):
                        mm = pe.matmul(side[:, b, t * P:(t + 1) * P], lhs[:, t * P:(t + 1) * P], w_proj[:, w, :],
                                       start=True, stop=True)
                    mm.then_inc(s_v_psum if name == "v" else s_out_psum, 1)
                elif name.endswith("_up"):
                    pe.wait_ge(s_lo[which], index + 1)
                    for n, part in enumerate((x_hi, x_lo)):
                        mm = pe.matmul(side[:, b, :], w1_q[:, arg * P:(arg + 1) * P], part[:], start=(n == 0), stop=(n == 1))
                    mm.then_inc(s_up[which], 1)
                elif name.endswith("_down"):
                    if arg == 0:
                        pe.wait_ge(s_hid[which], (index + 1) * FT)
                    for n in range(FT):
                        mm = pe.matmul(side[:, b, arg * P:(arg + 1) * P], hidden[:, n, arg * P:(arg + 1) * P],
                                       w2_q[:, n, :], start=(n == 0), stop=(n == FT - 1))
                    if arg == T - 1:
                        mm.then_inc(s_down[which], 1)

            pe.wait_ge(s_abs, 2)
            pe.wait_ge(s_ones, 1)
            pe.matmul(side[:, 0, 0:2], ones_f[:], abs_sum[:], start=True, stop=True).then_inc(s_gamma, 1)
            pe.wait_ge(s_thr, 1)
            pe.wait_ge(s_wq, 2)
            pe.wait_ge(s_ident_b, 1)
            pe.wait_ge(s_ident, 16)
            pe.wait_ge(s_const, 16 * CONST_DMAS)
            for use in PROLOGUE:
                side_work(use)
            for s in range(LEAD):
                scores_of(0, s, (0, 1, 2, 3))
                if s == QUAD:
                    side_work(("max_T", 0, 0, 0))
            for ph in phases(pe.Fori):
                i = ph.i
                if not isinstance(i, int) or i > 0:
                    last[:] = [Phase(i - 1, **(LAST if ph.i is B else {})).last_side(b) for b in range(2)]
                for s in range(H):
                    ahead = ph.core and (s < H - LEAD or ph.next_max)
                    ia, sa = (i, s + LEAD) if s < H - LEAD else (i + 1, s + LEAD - H)
                    def scores_pair(t):
                        if ph.core:
                            scores_T_of(i, s, t)
                        if ahead:
                            scores_of(ia, sa, (t,))

                    scores_pair(0)
                    if ph.core:
                        scores_T_of(i, s, 1)
                    side_work(ph.side(s, 0))
                    if ahead:
                        scores_of(ia, sa, (1,))
                    if ph.post if s < QUAD else ph.core:
                        values(i * NQ + (s // QUAD - 1), (s // QUAD - 1) % NQ, s % QUAD)
                    if ahead:
                        scores_of(ia, sa, (2,))
                    if ph.core:
                        scores_T_of(i, s, 2)
                    side_work(ph.side(s, 1))
                    scores_pair(3)
                    side_work(ph.side(s, 2))

        @block.scalar
        def _(act):
            def side_part(use):
                if use is None:
                    return
                name, arg, index, b = use
                which = name.split("_")[0]
                if name == "max_T":
                    act.wait_ge(s_maxT_psum, index + 1)
                    wait(act, s_maxrow, index * 16)
                    act.activation(max_T[:], side[:, b, :].bitcast(BF16)[0:PARTS * QUAD * T, 0:P], ACT.Copy).then_inc(s_maxT, 1)
                elif name == "attn_T":
                    act.wait_ge(s_T["attn"], index + 1)
                    act.activation(x_T[:], side[:, b, :], ACT.Copy).then_inc(s_xT, 1)
                elif name in ("ffn1_T", "ffn2_T"):
                    act.wait_ge(s_T[which], index + 1)
                    act.activation(x_hi[:], side[:, b, :], ACT.Copy).then_inc(s_hi[which], 1)
                elif name in ("q", "k"):
                    act.wait_ge(s_qk_psum[name], index + 1)
                    wait(act, s_rope[name], index * ROPE_STEPS)
                    n = "qk".index(name)
                    act.activation(qk[name][:], side[:, b, :], ACT.Identity, bias=bqk_col[:, n:n + 1]).then_inc(s_qk[name], 1)
                elif name.endswith("_up"):
                    act.wait_ge(s_up[which], index * FT + (arg + 1))
                    act.activation(hidden[:, arg, :], side[:, b, :], ACT.Relu, bias=b1_col[:, arg:arg + 1]).then_inc(s_hid[which], 1)
                elif name == "out_T":
                    act.wait_ge(s_outT_psum, index + 1)
                    act.activation(attn_T[:], side[:, b, :], ACT.Copy).then_inc(s_outT, 1)

            def exps(i, s, t):
                n = s * T + t
                if s % QUAD == 0 and t == 0:
                    wait(act, s_pv, i * NQ + (s // QUAD - 1))
                act.wait_ge(s_scoresT, i * (H * T) + (n + 1))
                act.activation(probs[:, s % (2 * QUAD), t, :], scores_T[:, bank_of(n, NST), :], ACT.Exp,
                               scale=SCALE).then_inc(s_exp, 1)

            def take_heads(quad):
                act.wait_ge(s_pv, quad + 1)
                wait(act, s_headsT, quad)
                act.activation(heads[:], heads_acc[:], ACT.Copy).then_inc(s_heads, 1)

            act.wait_ge(s_w1, 16)
            act.activation(hidden[:, 0, :], w1_raw[:], ACT.Abs, accum_out=abs_sum[:, 0:1]).then_inc(s_abs, 1)
            act.wait_ge(s_w2, 16)
            act.activation(hidden[:, 1, :], w2_raw[:].rearrange("p n d -> p (n d)"), ACT.Abs,
                           accum_out=abs_sum[:, 1:2]).then_inc(s_abs, 1)
            act.wait_ge(s_const, 16 * CONST_DMAS)
            for use in PROLOGUE:
                side_part(use)
            side_part(("max_T", 0, 0, 0))
            for ph in phases(act.Fori):
                i = ph.i
                for s in range(H):
                    if s % QUAD == 0 and (ph.post if s < 2 * QUAD else ph.core):
                        take_heads(i * NQ + (s // QUAD - 2))
                    if ph.core:
                        exps(i, s, 0)
                    if ph.core:
                        exps(i, s, 1)
                    side_part(ph.side(s, 0))
                    if ph.core:
                        exps(i, s, 2)
                    side_part(ph.side(s, 1))
                    if ph.core:
                        exps(i, s, 3)
                    side_part(ph.side(s, 2))

        @block.vector
        def _(dve):
            def ln_stats(n, j):
                if n == "ffn1":
                    dve.wait_ge(*((s_x0, 16) if isinstance(j, int) and j == 0 else (s_x, 16 * (B - 1))))
                else:
                    alone(dve, "dve", s_x1 if n == "attn" else s_x2, j + 1)
                for t in range(T):
                    dve.bn_stats(stats[n][:, t, :], tile_rows(j, t)).then_inc(s_stats[n], 1)
                alone(dve, "dve", s_stats[n], (j + 1) * T)
                for t in range(T):
                    dve.bn_aggr(mean_var[n][:, t, :], stats[n][:, t, :]).then_inc(s_var[n], 1)

            def ln_apply(n, j, tiles):
                if 0 in tiles:
                    dve.wait_ge(s_rstd[n], j + 1)
                    dve.wait_ge(s_var[n], (j + 1) * T)
                    wait(dve, s_T[n], j)
                for t in tiles:
                    dve.tensor_scalar(normed[n][:, t, :], tile_rows(j, t), mean_var[n][:, t, 0:1],
                                      rstd[n][:, t:t + 1], ALU.subtract, ALU.mult).then_inc(s_normed[n], 1)

            def norm(use):
                if use is not None:
                    what, n, j = use
                    if what == "stats":
                        ln_stats(n, j)
                    else:
                        ln_apply(n, j, {"apply": range(T), "apply_first": range(T // 2),
                                        "apply_rest": range(T // 2, T)}[what])

            def max_of(i, s, tiles):
                for t in tiles:
                    dve.wait_ge(s_scores, (i * H + s) * T + (t + 1))
                    if s % QUAD == 0 and t == 0:
                        wait(dve, s_split, (i * NQ + s // QUAD) * SPLIT_STEPS)
                    c = (s % QUAD) * T + t
                    dve.tensor_reduce(maxima[:, c:c + 1], scores[:, bank_of(s * T + t, NSC), :], AX_X, ALU.max).then_inc(s_max, 1)

            def split_max(quad):
                n = quad * SPLIT_STEPS
                dve.wait_ge(s_max, (quad + 1) * (QUAD * T))
                wait(dve, s_maxT_psum, quad)
                dve.tensor_copy(max_parts[:, 0, :], maxima[:]).then_inc(s_split, 1)
                dve.wait_ge(s_split, n + 1)
                dve.tensor_tensor(max_rest[:], maxima[:], max_parts[:, 0, :], ALU.subtract).then_inc(s_split, 1)
                dve.wait_ge(s_split, n + 2)
                dve.tensor_copy(max_parts[:, 1, :], max_rest[:]).then_inc(s_split, 1)
                dve.wait_ge(s_split, n + 3)
                dve.tensor_tensor(max_rest2[:], max_rest[:], max_parts[:, 1, :], ALU.subtract).then_inc(s_split, 1)
                dve.wait_ge(s_split, n + 4)
                dve.tensor_copy(max_parts[:, 2, :], max_rest2[:]).then_inc(s_split, 1)

            def side_part(use):
                if use is None:
                    return
                name, arg, index, b = use
                which = name.split("_")[0]
                if name == "heads_T":
                    per_head = side[:, b, :].rearrange("p (t j c) -> p t j c", t=T, j=QUAD)
                    g = arg
                    dve.wait_ge(s_headsT, index + 1)
                    dve.reciprocal(sums_inv[:], per_head[:, :, :, DH]).then_inc(s_inv, 1)
                    dve.wait_ge(s_inv, index + 1)
                    dve.tensor_tensor(attn_out[:, :, g * QUAD:(g + 1) * QUAD, :], per_head[:, :, :, 0:DH],
                                      sums_inv[:].unsqueeze(3).to_broadcast([P, T, QUAD, DH]),
                                      ALU.mult).then_inc(s_attn, 1)
                elif name in ("ffn1_T", "ffn2_T"):
                    dve.wait_ge(s_hi[which], index + 1)
                    dve.tensor_tensor(x_lo[:], side[:, b, :], x_hi[:], ALU.subtract).then_inc(s_lo[which], 1)
                elif name == "v":
                    dve.wait_ge(s_v_psum, index + 1)
                    wait(dve, s_v_heads, index * NQ)
                    dve.tensor_tensor(v_next[:], side[:, b, :].rearrange("p (t d) -> p t d", t=T), rows[:, 0:1, :].to_broadcast([P, T, D]),
                                      ALU.add).then_inc(s_v_next, 1)
                elif name == "out":
                    dve.wait_ge(s_out_psum, index + 1)
                    dve.wait_ge(s_xb["out"], index + 1)
                    dve.tensor_tensor(batch_rows(index), side[:, b, :].rearrange("p (t d) -> p t d", t=T), xb["out"][:], ALU.add).then_inc(s_x2, 1)
                elif name.endswith("_down") and arg == T - 1:
                    dve.wait_ge(s_down[which], index + 1)
                    dve.wait_ge(s_xb[which], index + 1)
                    dve.tensor_tensor(batch_rows(index), side[:, b, :].rearrange("p (t d) -> p t d", t=T), xb[which][:], ALU.add)\
                       .then_inc(s_x1 if which == "ffn1" else s_y, 1)

            dve.memset(ones_f[:], 1.0).then_inc(s_ones, 1)
            dve.memset(minus_half[:], -0.5).then_inc(s_minus_half, 1)
            norm(("stats", "ffn1", 0))
            dve.memset(k_stack[64:96, :, :], -1.0).then_inc(s_k_fill, 1)
            dve.wait_ge(s_ident, 16)
            dve.tensor_copy(ident_b[:], ident_f[:]).then_inc(s_ident_b, 1)
            dve.wait_ge(s_b2, 16)
            dve.tensor_scalar(b2_half[:], rows[:, 2:3, :], 0.5, None, ALU.mult).then_inc(s_b2h, 1)
            norm(("apply", "ffn1", 0))
            dve.wait_ge(s_gamma, 1)
            dve.tensor_scalar(thr[:, 0, :], side[:, 0, 0:2], 1.0 / (F * D), Q_EPS, ALU.mult, ALU.add).then_inc(s_thr, 1)
            dve.wait_ge(s_thr, 1)
            dve.tensor_scalar(thr[:, 1, :], thr[:, 0, :], 0.5, None, ALU.mult).then_inc(s_thr, 1)
            dve.tensor_scalar(thr[:, 2, :], thr[:, 0, :], -0.5, None, ALU.mult).then_inc(s_thr, 1)
            dve.wait_ge(s_thr, 3)
            dve.tensor_scalar(is_low[:], w1_raw[:], thr[:, 2, 0:1], None, ALU.is_lt).then_inc(s_thr, 1)
            dve.wait_ge(s_thr, 4)
            dve.scalar_tensor_tensor(out=w1_q[:], in0=w1_raw[:], scalar=thr[:, 1, 0:1], in1=is_low[:],
                                     op0=ALU.is_gt, op1=ALU.subtract).then_inc(s_wq, 1)
            dve.wait_ge(s_wq, 1)
            w2_flat = w2_raw[:].rearrange("p n d -> p (n d)")
            dve.tensor_scalar(is_low[:], w2_flat, thr[:, 2, 1:2], 0.5, ALU.is_lt, ALU.mult).then_inc(s_thr, 1)
            dve.tensor_scalar(is_high[:], w2_flat, thr[:, 1, 1:2], 0.5, ALU.is_gt, ALU.mult).then_inc(s_thr, 1)
            dve.wait_ge(s_thr, 6)
            dve.tensor_tensor(w2_q[:].rearrange("p n d -> p (n d)"), is_high[:], is_low[:], ALU.subtract).then_inc(s_wq, 1)
            dve.wait_ge(s_const, 16 * CONST_DMAS)
            dve.memset(v_heads[:], 0.0).then_inc(s_v_fill, 1)
            dve.wait_ge(s_v_fill, 1)
            dve.memset(v_heads[:, :, :, DH], 1.0).then_inc(s_v_fill, 1)
            for use in PROLOGUE:
                side_part(use)
                if use[0] == "ffn1_down" and use[1] == T - 1:
                    norm(("stats", "attn", use[2]))
                    norm(("apply", "attn", use[2]))
                    if use[2] == 0:
                        norm(("stats", "ffn1", 1))
                        norm(("apply", "ffn1", 1))
            for s in range(LEAD):
                max_of(0, s, (0, 1, 2, 3))
                if s == QUAD - 1:
                    split_max(0)
            for ph in phases(dve.Fori):
                i = ph.i
                for s in range(H):
                    ahead = ph.core and (s < H - LEAD or ph.next_max)
                    ia, sa = (i, s + LEAD) if s < H - LEAD else (i + 1, s + LEAD - H)
                    if ahead:
                        max_of(ia, sa, (0,))
                    side_part(ph.side(s, 0))
                    norm(ph.ln(s, 0))
                    if ahead:
                        max_of(ia, sa, (1, 2))
                    side_part(ph.side(s, 1))
                    norm(ph.ln(s, 1))
                    if ahead:
                        max_of(ia, sa, (3,))
                        if sa % QUAD == QUAD - 1:
                            split_max(ia * NQ + sa // QUAD)
                    side_part(ph.side(s, 2))
                    norm(ph.ln(s, 2))

        @block.gpsimd
        def _(pool):
            def inv_std(n, j):
                pool.wait_ge(s_var[n], (j + 1) * T)
                alone(pool, "pool", s_normed[n], j * T)
                pool.tensor_scalar(var_eps[n][:], mean_var[n][:, :, 1], LN_EPS, None, ALU.add).then_inc(s_vareps[n], 1)
                pool.wait_ge(s_vareps[n], j + 1)
                pool.tensor_tensor(rstd[n][:], var_eps[n][:], minus_half[:], ALU.pow).then_inc(s_rstd[n], 1)

            def add_bias(n, j):
                ready, used, bias = {"ffn1": (None, s_x1, b2_half[:]), "out": (s_x1, s_x2, rows[:, 1:2, :]),
                                     "ffn2": (s_x2, s_y, b2_half[:])}[n]
                if ready is None:
                    pool.wait_ge(*((s_x0, 16) if isinstance(j, int) and j == 0 else (s_x, 16 * (B - 1))))
                else:
                    pool.wait_ge(ready, j + 1)
                alone(pool, "pool", used, j)
                pool.tensor_tensor(xb[n][:], batch_rows(j), bias.to_broadcast([P, T, D]), ALU.add).then_inc(s_xb[n], 1)

            def rotate(n, j):
                done = j * ROPE_STEPS
                pool.wait_ge(s_qk[n], j + 1)
                other, count = ("q", done) if n == "k" else ("k", done + ROPE_STEPS)
                wait(pool, s_rope[other], count)
                pool.tensor_tensor(rope_a[:], qk[n][:], cos_t[:], ALU.mult).then_inc(s_rope[n], 1)
                pool.wait_ge(s_swap[n], (j + 1) * 32)
                pool.tensor_tensor(rope_b[:], qk_swap[n][:], sin_t[:], ALU.mult).then_inc(s_rope[n], 1)
                pool.wait_ge(s_rope[n], done + 2)
                pool.tensor_tensor(rope_a[:], rope_a[:], rope_b[:], ALU.add).then_inc(s_rope[n], 1)
                pool.wait_ge(s_rope[n], done + 3)
                alone(pool, "pool", s_scratch[n], j * 16)
                pool.tensor_scalar(qk_parts[n][:, 0, :], rope_a[:], 1.0, 0.0, ALU.mult, ALU.add).then_inc(s_rope[n], 1)
                pool.wait_ge(s_rope[n], done + 4)
                pool.tensor_tensor(rope_b[:], rope_a[:], qk_parts[n][:, 0, :], ALU.subtract).then_inc(s_rope[n], 1)
                alone(pool, "pool", s_rope[n], done + 5)
                pool.tensor_scalar(qk_parts[n][:, 1, :], rope_b[:], 1.0, 0.0, ALU.mult, ALU.add).then_inc(s_rope[n], 1)
                pool.wait_ge(s_rope[n], done + 6)
                pool.tensor_tensor(qk_parts[n][:, 2, :], rope_b[:], qk_parts[n][:, 1, :], ALU.subtract).then_inc(s_rope[n], 1)

            def fill_values(j, g):
                pool.wait_ge(s_v_next, j + 1)
                alone(pool, "pool", s_pv, j * NQ + (g + 1 - NQ))
                pool.tensor_scalar(v_heads[:, :, g * QUAD:(g + 1) * QUAD, 0:DH],
                                   v_next[:].rearrange("p t (h c) -> p t h c", h=H)[:, :, g * QUAD:(g + 1) * QUAD, :],
                                   1.0, 0.0, ALU.mult, ALU.add).then_inc(s_v_heads, 1)

            pool.wait_ge(s_minus_half, 1)
            inv_std("ffn1", 0)
            pool.wait_ge(s_b2h, 1)
            add_bias("ffn1", 0)
            inv_std("attn", 0)
            inv_std("ffn1", 1)
            add_bias("ffn1", 1)
            pool.wait_ge(s_const, 16 * CONST_DMAS)
            rotate("k", 0)
            rotate("q", 0)
            pool.wait_ge(s_v_fill, 2)
            fill_values(0, 0)
            fill_values(0, 1)
            inv_std("attn", 1)
            for ph in phases(pool.Fori):
                i = ph.i
                if ph.core:
                    fill_values(i, 2)
                if ph.post:
                    add_bias("out", i - 1)
                if ph.ffn1:
                    inv_std("ffn1", i + 2)
                if ph.proj:
                    rotate("k", i + 1)
                if ph.core:
                    fill_values(i, 3)
                if ph.proj:
                    rotate("q", i + 1)
                if ph.ffn1:
                    add_bias("ffn1", i + 2)
                if ph.post:
                    inv_std("ffn2", i - 1)
                    add_bias("ffn2", i - 1)
                if ph.ffn1:
                    inv_std("attn", i + 2)
                if ph.proj:
                    fill_values(i + 1, 0)
                    fill_values(i + 1, 1)


def kernel(**inputs):
    import concourse.bacc as bacc
    from concourse.bass_utils import run_bass_kernel_spmd

    def given(name, transpose=False):
        a = np.asarray(inputs[name])
        return np.ascontiguousarray(a.T if transpose else a)

    position = (np.arange(P)[None, :] * T + np.arange(T)[:, None]).reshape(-1).astype(np.float32)
    channel = np.arange(D) % DH
    inv_freq = (1.0 / np.float32(10000.0) ** (np.arange(0, DH, 2, dtype=np.float32) / np.float32(DH))).astype(np.float32)
    theta = (position[None, :] * inv_freq[channel // 2][:, None]).astype(np.float32)
    sign = np.where(channel % 2 == 0, -1.0, 1.0).astype(np.float32)[:, None]
    arrays = {
        "x": given("L0_attn_x"),
        "wq": given("L0_attn_Wq", True), "bq": given("L0_attn_bq").reshape(D, 1),
        "wk": given("L0_attn_Wk", True), "bk": given("L0_attn_bk").reshape(D, 1),
        "wv": given("L0_attn_Wv", True), "bv": given("L0_attn_bv"),
        "wo": given("L0_attn_Wo", True), "bo": given("L0_attn_bo"),
        "w1": given("L0_ffn_W1", True), "b1": np.ascontiguousarray(given("L0_ffn_b1").reshape(FT, P).T),
        "w2": given("L0_ffn_W2", True), "b2": given("L0_ffn_b2"),
        "ident": np.eye(P, dtype=np.float32),
        "rope_cos": np.cos(theta), "rope_sin": sign * np.sin(theta),
    }
    nc = bacc.Bacc("TRN2", target_bir_lowering=False, num_devices=1)
    args = [nc.dram_tensor(f"in_{n}", a.shape, mybir.dt.from_np(a.dtype), kind="ExternalInput").ap()
            for n, a in arrays.items()]
    out = nc.dram_tensor("out_y", (B, S, D), F32, kind="ExternalOutput").ap()
    macaron_layer(nc, *args, out)
    r = run_bass_kernel_spmd(nc, [{f"in_{n}": a for n, a in arrays.items()}], core_ids=[0])
    return r.results[0]["out_y"]
```

```python
from contextlib import ExitStack

import numpy as np

import concourse.bass as bass
from concourse import mybir

ALU = mybir.AluOpType
ACT = mybir.ActivationFunctionType
AX_X = mybir.AxisListType.X
F32 = mybir.dt.float32
F16 = mybir.dt.float16
BF16 = mybir.dt.bfloat16

P = 128
B, S, D = 8, 512, 128
H = 16
DH = D // H
F = 512
T = S // P
FT = F // P
NST = 2
NSC = 3
QUAD = 4
NQ = H // QUAD
LEAD = 7
PARTS = 3
ROWS = PARTS * PARTS * DH
LN_EPS = 1e-5
Q_EPS = 1e-5
SCALE = float(DH) ** -0.5
STACK_DMAS = 1 + PARTS
STACK_LANDED = 16 * STACK_DMAS

SIDE = {
    (0, 0): ("attn_T", 0, 0), (0, 2): ("heads_T", 0, 1),
    (1, 0): ("k", 0, 0), (1, 2): ("max_T", 0, 1),
    (2, 1): ("q", 0, 0), (2, 2): ("ffn1_T", 0, 1),
    (3, 1): ("ffn1_up", 0, 1), (3, 2): ("ffn1_up", 1, 0),
    (4, 0): ("ffn1_up", 2, 1), (4, 1): ("ffn1_up", 3, 0), (4, 2): ("heads_T", 0, 1),
    (5, 0): ("ffn1_down", 0, 0), (5, 1): ("out_T", 0, 1), (5, 2): ("ffn1_down", 1, 0),
    (6, 0): ("max_T", 0, 1), (6, 1): ("out", 0, 1), (6, 2): ("ffn1_down", 2, 0),
    (7, 2): ("ffn1_down", 3, 0),
    (8, 1): ("heads_T", 0, 1), (8, 2): ("ffn2_T", 0, 0),
    (9, 1): ("ffn2_up", 0, 1), (9, 2): ("max_T", 0, 0),
    (10, 0): ("ffn2_up", 1, 1), (10, 1): ("ffn2_up", 2, 0), (10, 2): ("ffn2_up", 3, 1),
    (11, 1): ("ffn2_down", 0, 0),
    (12, 0): ("ffn2_down", 1, 0), (12, 2): ("heads_T", 0, 1),
    (13, 1): ("max_T", 0, 1), (13, 2): ("ffn2_down", 2, 0),
    (14, 2): ("ffn2_down", 3, 0),
    (15, 1): ("v", 0, 0),
}
LN = {
    (0, 0): ("stats", "ffn1"), (1, 2): ("apply_first", "ffn1"), (2, 0): ("apply_rest", "ffn1"),
    (6, 1): ("stats", "ffn2"), (7, 2): ("apply_first", "ffn2"), (8, 0): ("apply_rest", "ffn2"),
    (10, 2): ("stats", "attn"), (14, 0): ("apply_first", "attn"), (14, 1): ("apply_rest", "attn"),
}


class Phase:

    def __init__(self, i, core=True, next_max=True, ffn1=True, proj=True, post=True):
        self.i, self.core, self.next_max, self.ffn1, self.proj, self.post = i, core, next_max, ffn1, proj, post

    def batch(self, kind):
        return self.i + {"ffn1": 2, "proj": 1, "post": -1}[kind]

    def side(self, step, slot):
        found = SIDE.get((step, slot))
        if found is None:
            return None
        name, arg, bank = found
        if name == "max_T":
            quad = self.i * NQ + (step // QUAD + 1)
            on = self.core and (step < H - QUAD or self.next_max)
            return (name, arg, quad, bank) if on else None
        if name == "heads_T":
            quad = self.i * NQ + step // QUAD - 2
            on = self.post if step < 2 * QUAD else self.core
            return (name, (step // QUAD - 2) % NQ, quad, bank) if on else None
        kind = {"ffn1": "ffn1", "ffn2": "post", "out": "post"}.get(name.split("_")[0], "proj")
        on = {"ffn1": self.ffn1, "proj": self.proj, "post": self.post}[kind]
        return (name, arg, self.batch(kind), bank) if on else None

    def ln(self, step, slot):
        found = LN.get((step, slot))
        if found is None:
            return None
        what, which = found
        kind = {"ffn1": "ffn1", "attn": "ffn1", "ffn2": "post"}[which]
        on = {"ffn1": self.ffn1, "post": self.post}[kind]
        return (what, which, self.batch(kind)) if on else None

    def ahead(self, step):
        if not self.core or (step >= H - LEAD and not self.next_max):
            return None
        return (self.i, step + LEAD) if step < H - LEAD else (self.i + 1, step + LEAD - H)

    def last_side(self, bank):
        found = [self.side(s, c) for s in range(H) for c in range(3)]
        return [x for x in found if x and x[3] == bank][-1]


def first_ffn(j):
    return ([("ffn1_T", 0, j, 0)] + [("ffn1_up", n, j, 1 - n % 2) for n in range(FT)]
            + [("ffn1_down", n, j, 1) for n in range(T)])


PROLOGUE = (first_ffn(0) + [("attn_T", 0, 0, 0), ("k", 0, 0, 1), ("q", 0, 0, 0), ("v", 0, 0, 1)] + first_ffn(1))
FILL = {("sums", 0, 0): 20, ("ffn1_T", 0, 0): 4, ("ffn1_up", 0, 0): 8, ("attn_T", 0, 0): 20, ("k", 0, 0): 6,
        ("v", 0, 0): 6, ("ffn1_up", 0, 1): 20, ("ffn1_down", 0, 1): 4,
        ("out_T", 0, B - 1): 6, ("out", 0, B - 1): 6, ("ffn2_T", 0, B - 1): 36, ("ffn2_up", 0, B - 1): 12,
        ("ffn2_down", 0, B - 1): 6}
FILL_BEFORE_SCORES = 32
FILL_BETWEEN_SCORES = 2
FILL_BEFORE_FIRST_STEP = 20
FILL_FIRST_STEPS = 3
FIRST = dict(post=False)
BEFORE_LAST = dict(ffn1=False)
LAST = dict(next_max=False, ffn1=False, proj=False)
DRAIN = dict(core=False, next_max=False, ffn1=False, proj=False)
LOOP = (2, B - 2)


def wait(engine, semaphore, value):
    if not isinstance(value, int) or value > 0:
        engine.wait_ge(semaphore, value)


def phases(loop):
    yield Phase(0, **FIRST)
    yield Phase(1)
    with loop(*LOOP) as i:
        yield Phase(i)
    yield Phase(B - 2, **BEFORE_LAST)
    yield Phase(B - 1, **LAST)
    yield Phase(B, **DRAIN)


def macaron_layer(nc, x, wq, bq, wk, bk, wv, bv, wo, bo, w1, b1, w2, b2, ident, rope_cos, rope_sin, out):
    with ExitStack() as ctx:
        def sb(name, shape, dt=F32):
            return ctx.enter_context(nc.sbuf_tensor(name, shape, dt))

        def psum(name, shape, dt=F32):
            return ctx.enter_context(nc.psum_tensor(name, shape, dt))

        def sem(name):
            return ctx.enter_context(nc.semaphore(name))

        resid = sb("resid", [P, B * T, D])
        probs = sb("probs", [P, 2 * QUAD, T, S])
        q_stack = sb("q_stack", [P, H, S], BF16)
        k_stack = sb("k_stack", [P, H, S], BF16)
        v_heads = sb("v_heads", [P, T, H, 32])
        v_next = sb("v_next", [P, T, D])
        hidden = sb("hidden", [P, FT, S])
        w1_raw = sb("w1_raw", [P, F])
        w2_raw = sb("w2_raw", [P, FT, D])
        w1_q = sb("w1_q", [P, F], F16)
        w2_q = sb("w2_q", [P, FT, D])
        w_proj = sb("w_proj", [P, 4, D])
        b1_col = sb("b1_col", [P, FT])
        bqk_col = sb("bqk_col", [P, 2])
        rows = sb("rows", [P, 3, D])
        b2_half = sb("b2_half", [P, 1, D])
        ident_f = sb("ident_f", [P, P])
        ident_b = sb("ident_b", [P, P], BF16)
        ones_f = sb("ones_f", [P, P])
        cos_t = sb("cos_t", [P, S])
        sin_t = sb("sin_t", [P, S])
        abs_sum = sb("abs_sum", [P, 2])
        thr = sb("thr", [P, 3, 2])
        is_low = sb("is_low", [P, F])
        is_high = sb("is_high", [P, F])
        minus_half = sb("minus_half", [P, T])
        normed = {n: sb(f"normed_{n}", [P, T, D]) for n in ("ffn1", "attn", "ffn2")}
        stats = {n: sb(f"stats_{n}", [P, T, 6]) for n in normed}
        mean_var = {n: sb(f"mean_var_{n}", [P, T, 2]) for n in normed}
        var_eps = {n: sb(f"var_eps_{n}", [P, T]) for n in normed}
        rstd = {n: sb(f"rstd_{n}", [P, T]) for n in normed}
        xb = {n: sb(f"xb_{n}", [P, T, D]) for n in ("ffn1", "out", "ffn2")}
        x_hi = sb("x_hi", [P, S], F16)
        x_lo = sb("x_lo", [P, S], F16)
        x_T = sb("x_T", [P, S])
        qk = {n: sb(f"{n}_32", [P, S]) for n in "qk"}
        qk_swap = {n: sb(f"{n}_swap", [P, S]) for n in "qk"}
        qk_parts = {n: sb(f"{n}_parts", [P, PARTS, S], BF16) for n in "qk"}
        rope_a = sb("rope_a", [P, S])
        rope_b = sb("rope_b", [P, S])
        maxima = sb("maxima", [P, QUAD * T])
        max_rest = sb("max_rest", [P, QUAD * T])
        max_rest2 = sb("max_rest2", [P, QUAD * T])
        max_parts = sb("max_parts", [P, PARTS, QUAD * T], BF16)
        max_T = sb("max_T", [PARTS * QUAD * T, P], BF16)
        heads = sb("heads", [P, S])
        sums_inv = sb("sums_inv", [P, T, QUAD])
        attn_out = sb("attn_out", [P, T, H, DH])
        attn_T = sb("attn_T", [P, S])

        scores_T = psum("scores_T", [P, NST, S])
        scores = psum("scores", [P, NSC, S])
        heads_acc = psum("heads_acc", [P, S])
        side = psum("side", [P, 2, S])

        scratch = {n: nc.dram_tensor(f"{n}_scratch", [DH, PARTS, H, S], BF16, kind="Internal").ap() for n in "qk"}

        s_x0 = sem("x0_landed")
        s_x = sem("x_landed")
        s_ident = sem("ident_landed")
        s_w1 = sem("w1_landed")
        s_w2 = sem("w2_landed")
        s_b1 = sem("b1_landed")
        s_const = sem("consts_landed")
        s_minus_half = sem("minus_half_set")
        s_ones = sem("ones_set")
        s_k_fill = sem("k_stack_filled")
        s_v_fill = sem("v_heads_filled_with_constants")
        s_b2 = sem("b2_landed")
        s_b2h = sem("b2_half_ready")
        s_ident_b = sem("ident_b_ready")
        s_abs = sem("abs_sum_ready")
        s_gamma = sem("gamma_in_psum")
        s_thr = sem("thresholds_done")
        s_wq = sem("weights_quantised")
        s_stats = {n: sem(f"stats_done_{n}") for n in normed}
        s_var = {n: sem(f"var_ready_{n}") for n in normed}
        s_vareps = {n: sem(f"var_eps_ready_{n}") for n in normed}
        s_rstd = {n: sem(f"rstd_ready_{n}") for n in normed}
        s_normed = {n: sem(f"normed_{n}_ready") for n in normed}
        s_xb = {n: sem(f"xb_{n}_ready") for n in xb}
        s_T = {n: sem(f"normed_T_{n}_in_psum") for n in normed}
        s_hi = {n: sem(f"x_hi_{n}_ready") for n in ("ffn1", "ffn2")}
        s_lo = {n: sem(f"x_lo_{n}_ready") for n in ("ffn1", "ffn2")}
        s_up = {n: sem(f"up_{n}_in_psum") for n in ("ffn1", "ffn2")}
        s_hid = {n: sem(f"hidden_{n}_ready") for n in ("ffn1", "ffn2")}
        s_down = {n: sem(f"down_{n}_in_psum") for n in ("ffn1", "ffn2")}
        s_x1 = sem("x1_ready")
        s_x2 = sem("x2_ready")
        s_y = sem("y_ready")
        s_xT = sem("x_T_ready")
        s_qk_psum = {n: sem(f"{n}_in_psum") for n in "qk"}
        s_qk = {n: sem(f"{n}_32_ready") for n in "qk"}
        s_swap = {n: sem(f"{n}_swap_landed") for n in "qk"}
        s_rope = {n: sem(f"{n}_rope_steps") for n in "qk"}
        s_scratch = {n: sem(f"{n}_scratch_landed") for n in "qk"}
        s_stack = sem("stack_landed")
        s_v_psum = sem("v_in_psum")
        s_v_next = sem("v_next_ready")
        s_v_heads = sem("v_heads_filled")
        s_scores = sem("scores_in_psum")
        s_max = sem("maxima_done")
        s_split = sem("max_split_steps")
        s_maxT_psum = sem("max_T_in_psum")
        s_maxT = sem("max_T_ready")
        s_maxrow = sem("max_rows_landed")
        s_scoresT = sem("scores_T_in_psum")
        s_exp = sem("probs_ready")
        s_pv = sem("heads_acc_done")
        s_heads = sem("heads_ready")
        s_headsT = sem("heads_T_in_psum")
        s_inv = sem("sums_inv_ready")
        s_attn = sem("attn_out_ready")
        s_outT_psum = sem("attn_T_in_psum")
        s_outT = sem("attn_T_ready")
        s_out_psum = sem("out_in_psum")
        s_stored = sem("y_stored")

        s_gate = {n: sem(f"gate_{n}") for n in ("sp", "pe", "dve", "pool")}

        def alone(engine, name, semaphore, value):
            if not isinstance(value, int) or value > 0:
                engine.wait_ge(semaphore, value)
                if not isinstance(value, int):
                    engine.sem_inc(s_gate[name])

        CONST_DMAS = 10
        SPLIT_STEPS = 5
        ROPE_STEPS = 7

        def side_read(name, arg, index, bank):
            if name == "max_T":
                return s_maxT, index + 1
            if name == "heads_T":
                return s_attn, index + 1
            if name in ("q", "k"):
                return s_qk[name], index + 1
            if name in ("ffn1_up", "ffn2_up"):
                return s_hid[name[:4]], index * FT + (arg + 1)
            if name in ("ffn1_T", "ffn2_T"):
                return s_lo[name[:4]], index + 1
            return {"attn_T": s_xT, "v": s_v_next, "out_T": s_outT, "out": s_x2,
                    "ffn1_down": s_x1, "ffn2_down": s_y}[name], index + 1

        block = ctx.enter_context(nc.Block())

        def bank_of(n, banks):
            return 1 if n == H * T - 1 and (n + 1) % banks == 1 else n % banks

        def bank_used(n, banks):
            last = n - 1
            while bank_of(last % (H * T), banks) != bank_of(n, banks):
                last -= 1
            return last + 1

        def batch_rows(j):
            return resid[:, bass.ds(j * T, T), :]

        def tile_rows(j, t):
            return resid[:, bass.ds(j * T + t, 1), :].rearrange("p o d -> p (o d)")

        def rotate_begin(engine, n, j):
            done = j * ROPE_STEPS
            engine.wait_ge(s_qk[n], j + 1)
            other, count = ("q", done) if n == "k" else ("k", done + ROPE_STEPS)
            wait(engine, s_rope[other], count)
            engine.tensor_tensor(rope_a[:], qk[n][:], cos_t[:], ALU.mult).then_inc(s_rope[n], 1)

        def rotate_end(engine, gate, n, j):
            done = j * ROPE_STEPS
            engine.wait_ge(s_swap[n], (j + 1) * 32)
            engine.tensor_tensor(rope_b[:], qk_swap[n][:], sin_t[:], ALU.mult).then_inc(s_rope[n], 1)
            engine.wait_ge(s_rope[n], done + 2)
            engine.tensor_tensor(rope_a[:], rope_a[:], rope_b[:], ALU.add).then_inc(s_rope[n], 1)
            engine.wait_ge(s_rope[n], done + 3)
            alone(engine, gate, s_scratch[n], j * 16)
            engine.tensor_scalar(qk_parts[n][:, 0, :], rope_a[:], 1.0, 0.0, ALU.mult, ALU.add).then_inc(s_rope[n], 1)
            engine.wait_ge(s_rope[n], done + 4)
            engine.tensor_tensor(rope_b[:], rope_a[:], qk_parts[n][:, 0, :], ALU.subtract).then_inc(s_rope[n], 1)
            alone(engine, gate, s_rope[n], done + 5)
            engine.tensor_scalar(qk_parts[n][:, 1, :], rope_b[:], 1.0, 0.0, ALU.mult, ALU.add).then_inc(s_rope[n], 1)
            engine.wait_ge(s_rope[n], done + 6)
            engine.tensor_tensor(qk_parts[n][:, 2, :], rope_b[:], qk_parts[n][:, 1, :], ALU.subtract).then_inc(s_rope[n], 1)

        @block.sync
        def _(sp):
            sp.dma_start(resid[:, 0:T, :], x[0].rearrange("(p t) d -> p t d", t=T)).then_inc(s_x0, 16)
            sp.dma_start(ident_f[:], ident).then_inc(s_ident, 16)
            sp.dma_start(b1_col[:], b1).then_inc(s_b1, 16)
            sp.dma_start(rows[:, 2, :], b2.partition_broadcast(P)).then_inc(s_b2, 16)
            for n, w in enumerate((wq, wk, wv, wo)):
                sp.dma_start(w_proj[:, n, :], w).then_inc(s_const, 16)
            for n, b in enumerate((bq, bk)):
                sp.dma_start(bqk_col[:, n:n + 1], b).then_inc(s_const, 16)
            sp.dma_start(cos_t[:], rope_cos).then_inc(s_const, 16)
            sp.dma_start(sin_t[:], rope_sin).then_inc(s_const, 16)
            for n, b in enumerate((bv, bo)):
                sp.dma_start(rows[:, n, :], b.partition_broadcast(P)).then_inc(s_const, 16)
            for j in range(1, B):
                sp.dma_start(resid[:, j * T:(j + 1) * T, :], x[j].rearrange("(p t) d -> p t d", t=T)).then_inc(s_x, 16)

            def swap(n, j):
                sp.wait_ge(s_qk[n], j + 1)
                sp.dma_start(qk_swap[n][0:P:2, :], qk[n][1:P:2, :]).then_inc(s_swap[n], 16)
                sp.dma_start(qk_swap[n][1:P:2, :], qk[n][0:P:2, :]).then_inc(s_swap[n], 16)

            def to_scratch(n, j):
                alone(sp, "sp", s_rope[n], (j + 1) * ROPE_STEPS)
                wait(sp, s_stack, j * (NQ * STACK_LANDED))
                sp.dma_start(scratch[n].rearrange("d c h t -> h d c t"), qk_parts[n][:]).then_inc(s_scratch[n], 16)

            def stack(j, g):
                hs = slice(g * QUAD, (g + 1) * QUAD)
                alone(sp, "sp", s_scratch["k"], (j + 1) * 16)
                alone(sp, "sp", s_scratch["q"], (j + 1) * 16)
                alone(sp, "sp", s_scoresT, j * (H * T) + T * (QUAD * (g + 1) - H))
                wait(sp, s_stack, (j * NQ + g) * STACK_LANDED)
                src = scratch["q"][:, :, hs, :].rearrange("d c h t -> (d c) (h t)")
                src = bass.AP(src.tensor, src.offset, [[0, PARTS]] + [list(y) for y in src.ap])
                sp.dma_start(q_stack[0:ROWS, hs, :].rearrange("p h t -> p (h t)"), src).then_inc(s_stack, 16)
                for a in range(PARTS):
                    src = scratch["k"][:, a, hs, :].rearrange("d h t -> d (h t)")
                    src = bass.AP(src.tensor, src.offset, [list(src.ap[0]), [0, PARTS], list(src.ap[1])])
                    rows_a = slice(a * DH * PARTS, (a + 1) * DH * PARTS)
                    sp.dma_start(k_stack[rows_a, hs, :].rearrange("p h t -> p (h t)"), src).then_inc(s_stack, 16)

            def max_row(i, g):
                alone(sp, "sp", s_maxT, i * NQ + (g + 1))
                wait(sp, s_maxrow, (i * NQ + g) * 16)
                sp.dma_start(q_stack[ROWS:ROWS + PARTS, g * QUAD:(g + 1) * QUAD, :], max_T[:]).then_inc(s_maxrow, 16)

            sp.wait_ge(s_k_fill, 1)
            swap("k", 0)
            swap("q", 0)
            to_scratch("k", 0)
            to_scratch("q", 0)
            for g in range(NQ):
                stack(0, g)
            max_row(0, 0)
            for ph in phases(sp.Fori):
                i = ph.i
                if ph.proj:
                    swap("k", i + 1)
                if ph.core:
                    max_row(i, 1)
                if ph.proj:
                    swap("q", i + 1)
                    to_scratch("k", i + 1)
                    to_scratch("q", i + 1)
                if ph.core:
                    max_row(i, 2)
                if ph.proj:
                    stack(i + 1, 0)
                    stack(i + 1, 1)
                if ph.core:
                    max_row(i, 3)
                if ph.proj:
                    stack(i + 1, 2)
                if ph.next_max:
                    max_row(i + 1, 0)
                if ph.post:
                    alone(sp, "sp", s_y, i)
                    sp.dma_start(out[bass.ds(i - 1, 1)].rearrange("b (p t) d -> p (b t) d", t=T),
                                 batch_rows(i - 1)).then_inc(s_stored, 16)
                if ph.proj:
                    stack(i + 1, 3)
            sp.wait_ge(s_stored, 16 * B)

        @block.tensor
        def _(pe):
            def scores_of(head, tiles):
                if head is None:
                    return
                i, s = head
                for t in tiles:
                    if s % QUAD == 0 and t == 0:
                        pe.wait_ge(s_stack, (i * NQ + (s // QUAD + 1)) * STACK_LANDED)
                    n = s * T + t
                    wait(pe, s_max, i * (H * T) + bank_used(n, NSC))
                    pe.matmul(scores[:, bank_of(n, NSC), :], q_stack[0:ROWS, s, t * P:(t + 1) * P], k_stack[0:ROWS, s, :],
                              start=True, stop=True).then_inc(s_scores, 1)

            def scores_T_of(i, s, t):
                n = s * T + t
                if s % QUAD == 0 and t == 0:
                    pe.wait_ge(s_maxrow, (i * NQ + (s // QUAD + 1)) * 16)
                wait(pe, s_exp, i * (H * T) + bank_used(n, NST))
                pe.matmul(scores_T[:, bank_of(n, NST), :], k_stack[0:ROWS + PARTS, s, t * P:(t + 1) * P],
                          q_stack[0:ROWS + PARTS, s, :], start=True, stop=True).then_inc(s_scoresT, 1)

            def values(quad, g, kt):
                if kt == 0:
                    pe.wait_ge(s_exp, (quad + 1) * (T * QUAD))
                    pe.wait_ge(s_v_heads, quad + 1)
                    wait(pe, s_heads, quad)
                for j in range(QUAD):
                    mm = pe.matmul(heads_acc[32 * j:32 * j + 32, :], v_heads[:, kt, g * QUAD + j, :],
                                   probs[:, (g % 2) * QUAD + j, kt, :], start=(kt == 0), stop=(kt == T - 1))
                if kt == T - 1:
                    mm.then_inc(s_pv, 1)

            last = [None, None]

            def side_work(use):
                if use is None:
                    return
                name, arg, index, b = use
                if last[b] is not None and not (name.endswith("_down") and arg):
                    pe.wait_ge(*side_read(*last[b]))
                last[b] = use
                which = name.split("_")[0]
                if name == "max_T":
                    alone(pe, "pe", s_split, (index + 1) * SPLIT_STEPS)
                    pe.transpose(side[:, b, :].bitcast(BF16)[0:PARTS * QUAD * T, 0:P], max_parts[:].rearrange("p c n -> p (c n)"),
                                 ident_b[:]).then_inc(s_maxT_psum, 1)
                elif name == "heads_T":
                    pe.wait_ge(s_heads, index + 1)
                    for t in range(T):
                        mm = pe.transpose(side[:, b, t * P:(t + 1) * P], heads[:, t * P:(t + 1) * P], ident_f[:])
                    mm.then_inc(s_headsT, 1)
                elif name == "out_T":
                    pe.wait_ge(s_attn, (index + 1) * NQ)
                    for t in range(T):
                        mm = pe.transpose(side[:, b, t * P:(t + 1) * P],
                                          attn_out[:, t, :, :].rearrange("p h d -> p (h d)"), ident_f[:])
                    mm.then_inc(s_outT_psum, 1)
                elif name in ("ffn1_T", "attn_T", "ffn2_T"):
                    pe.wait_ge(s_normed[which], (index + 1) * T)
                    for t in range(T):
                        mm = pe.transpose(side[:, b, t * P:(t + 1) * P], normed[which][:, t, :], ident_f[:])
                    mm.then_inc(s_T[which], 1)
                elif name in ("q", "k"):
                    pe.wait_ge(s_xT, index + 1)
                    pe.matmul(side[:, b, :], w_proj[:, "qk".index(name), :], x_T[:], start=True,
                              stop=True).then_inc(s_qk_psum[name], 1)
                elif name in ("v", "out"):
                    lhs, w = (x_T, 2) if name == "v" else (attn_T, 3)
                    pe.wait_ge(s_xT if name == "v" else s_outT, index + 1)
                    for t in range(T):
                        mm = pe.matmul(side[:, b, t * P:(t + 1) * P], lhs[:, t * P:(t + 1) * P], w_proj[:, w, :],
                                       start=True, stop=True)
                    mm.then_inc(s_v_psum if name == "v" else s_out_psum, 1)
                elif name.endswith("_up"):
                    pe.wait_ge(s_lo[which], index + 1)
                    for n, part in enumerate((x_hi, x_lo)):
                        mm = pe.matmul(side[:, b, :], w1_q[:, arg * P:(arg + 1) * P], part[:], start=(n == 0), stop=(n == 1))
                    mm.then_inc(s_up[which], 1)
                elif name.endswith("_down"):
                    if arg == 0:
                        pe.wait_ge(s_hid[which], (index + 1) * FT)
                    for n in range(FT):
                        mm = pe.matmul(side[:, b, arg * P:(arg + 1) * P], hidden[:, n, arg * P:(arg + 1) * P],
                                       w2_q[:, n, :], start=(n == 0), stop=(n == FT - 1))
                    if arg == T - 1:
                        mm.then_inc(s_down[which], 1)

            def fill(count):
                some = ones_f[:].bitcast(BF16)
                for _ in range(count):
                    pe.matmul(heads_acc[:, 0:2 * P], some[:, 0:P], some, start=True, stop=True)

            def post_fill(ph, use):
                if not ph.core and use is not None and use[0] != "heads_T":
                    fill(FILL.get(use[:3], 0))

            pe.wait_ge(s_ones, 1)
            fill(FILL["sums", 0, 0])
            pe.wait_ge(s_abs, 2)
            pe.matmul(side[:, 0, 0:2], ones_f[:], abs_sum[:], start=True, stop=True).then_inc(s_gamma, 1)
            pe.wait_ge(s_thr, 1)
            pe.wait_ge(s_ident, 16)
            for use in PROLOGUE:
                if use[:3] == ("ffn1_up", 0, 0):
                    pe.wait_ge(s_wq, 1)
                if use[:3] == ("ffn1_down", 0, 0):
                    pe.wait_ge(s_wq, 2)
                if use[0] == "k":
                    pe.wait_ge(s_const, 16 * CONST_DMAS)
                fill(FILL.get(use[:3], 0))
                side_work(use)
            fill(FILL_BEFORE_SCORES)
            for s in range(LEAD):
                for t in range(T):
                    scores_of((0, s), (t,))
                    fill(FILL_BETWEEN_SCORES)
                if s == QUAD:
                    pe.wait_ge(s_ident_b, 1)
                    side_work(("max_T", 0, 0, 0))
            fill(FILL_BEFORE_FIRST_STEP)
            for ph in phases(pe.Fori):
                i = ph.i
                if not isinstance(i, int) or i > 0:
                    last[:] = [Phase(i - 1, **(LAST if ph.i is B else {})).last_side(b) for b in range(2)]
                for s in range(H):
                    ahead = ph.ahead(s)
                    if ph.core:
                        scores_T_of(i, s, 0)
                    scores_of(ahead, (0,))
                    post_fill(ph, ph.side(s, 0))
                    side_work(ph.side(s, 0))
                    if ph.core:
                        scores_T_of(i, s, 1)
                    scores_of(ahead, (1,))
                    if s % QUAD == 0:
                        scores_of(ahead, (2,))
                    if ph.post if s < QUAD else ph.core:
                        values(i * NQ + (s // QUAD - 1), (s // QUAD - 1) % NQ, s % QUAD)
                    elif s < QUAD:
                        fill(FILL_FIRST_STEPS)
                    if s % QUAD:
                        scores_of(ahead, (2,))
                    if ph.core:
                        scores_T_of(i, s, 2)
                    post_fill(ph, ph.side(s, 1))
                    side_work(ph.side(s, 1))
                    if ph.core:
                        scores_T_of(i, s, 3)
                    scores_of(ahead, (3,))
                    post_fill(ph, ph.side(s, 2))
                    side_work(ph.side(s, 2))

        @block.scalar
        def _(act):
            def side_part(use):
                if use is None:
                    return
                name, arg, index, b = use
                which = name.split("_")[0]
                if name == "max_T":
                    act.wait_ge(s_maxT_psum, index + 1)
                    wait(act, s_maxrow, index * 16)
                    act.activation(max_T[:], side[:, b, :].bitcast(BF16)[0:PARTS * QUAD * T, 0:P], ACT.Copy).then_inc(s_maxT, 1)
                elif name == "attn_T":
                    act.wait_ge(s_T["attn"], index + 1)
                    act.activation(x_T[:], side[:, b, :], ACT.Copy).then_inc(s_xT, 1)
                elif name in ("ffn1_T", "ffn2_T"):
                    act.wait_ge(s_T[which], index + 1)
                    act.activation(x_hi[:], side[:, b, :], ACT.Copy).then_inc(s_hi[which], 1)
                elif name in ("q", "k"):
                    act.wait_ge(s_qk_psum[name], index + 1)
                    wait(act, s_rope[name], index * ROPE_STEPS)
                    n = "qk".index(name)
                    act.activation(qk[name][:], side[:, b, :], ACT.Identity, bias=bqk_col[:, n:n + 1]).then_inc(s_qk[name], 1)
                elif name.endswith("_up"):
                    act.wait_ge(s_up[which], index * FT + (arg + 1))
                    act.activation(hidden[:, arg, :], side[:, b, :], ACT.Relu, bias=b1_col[:, arg:arg + 1]).then_inc(s_hid[which], 1)
                elif name == "out_T":
                    act.wait_ge(s_outT_psum, index + 1)
                    act.activation(attn_T[:], side[:, b, :], ACT.Copy).then_inc(s_outT, 1)

            def exps(i, s, t):
                n = s * T + t
                if s % QUAD == 0 and t == 0:
                    wait(act, s_pv, i * NQ + (s // QUAD - 1))
                act.wait_ge(s_scoresT, i * (H * T) + (n + 1))
                act.activation(probs[:, s % (2 * QUAD), t, :], scores_T[:, bank_of(n, NST), :], ACT.Exp,
                               scale=SCALE).then_inc(s_exp, 1)

            def take_heads(quad):
                act.wait_ge(s_pv, quad + 1)
                wait(act, s_headsT, quad)
                act.activation(heads[:], heads_acc[:], ACT.Copy).then_inc(s_heads, 1)

            act.dma_start(w1_raw[:], w1).then_inc(s_w1, 16)
            act.dma_start(w2_raw[:], w2.rearrange("(n p) d -> p n d", p=P)).then_inc(s_w2, 16)
            act.wait_ge(s_w1, 16)
            act.activation(hidden[:, 0, :], w1_raw[:], ACT.Abs, accum_out=abs_sum[:, 0:1]).then_inc(s_abs, 1)
            act.wait_ge(s_w2, 16)
            act.activation(hidden[:, 1, :], w2_raw[:].rearrange("p n d -> p (n d)"), ACT.Abs,
                           accum_out=abs_sum[:, 1:2]).then_inc(s_abs, 1)
            act.wait_ge(s_b1, 16)
            for use in PROLOGUE:
                if use[0] == "k":
                    act.wait_ge(s_const, 16 * CONST_DMAS)
                side_part(use)
            side_part(("max_T", 0, 0, 0))
            for ph in phases(act.Fori):
                i = ph.i
                for s in range(H):
                    if s % QUAD == 0 and (ph.post if s < 2 * QUAD else ph.core):
                        take_heads(i * NQ + (s // QUAD - 2))
                    if ph.core:
                        exps(i, s, 0)
                    side_part(ph.side(s, 0))
                    if ph.core:
                        exps(i, s, 1)
                        exps(i, s, 2)
                    side_part(ph.side(s, 1))
                    if ph.core:
                        exps(i, s, 3)
                    side_part(ph.side(s, 2))

        @block.vector
        def _(dve):
            def ln_stats(n, j):
                if n == "ffn1":
                    dve.wait_ge(*((s_x0, 16) if isinstance(j, int) and j == 0 else (s_x, 16 * (B - 1))))
                else:
                    alone(dve, "dve", s_x1 if n == "attn" else s_x2, j + 1)
                for t in range(T):
                    dve.bn_stats(stats[n][:, t, :], tile_rows(j, t)).then_inc(s_stats[n], 1)
                alone(dve, "dve", s_stats[n], (j + 1) * T)
                for t in range(T):
                    dve.bn_aggr(mean_var[n][:, t, :], stats[n][:, t, :]).then_inc(s_var[n], 1)

            def ln_apply(n, j, tiles):
                if 0 in tiles:
                    dve.wait_ge(s_rstd[n], j + 1)
                    dve.wait_ge(s_var[n], (j + 1) * T)
                    wait(dve, s_T[n], j)
                for t in tiles:
                    dve.tensor_scalar(normed[n][:, t, :], tile_rows(j, t), mean_var[n][:, t, 0:1],
                                      rstd[n][:, t:t + 1], ALU.subtract, ALU.mult).then_inc(s_normed[n], 1)

            def norm(use):
                if use is not None:
                    what, n, j = use
                    if what == "stats":
                        ln_stats(n, j)
                    else:
                        ln_apply(n, j, {"apply": range(T), "apply_first": range(T // 2),
                                        "apply_rest": range(T // 2, T)}[what])

            def split_max(quad):
                n = quad * SPLIT_STEPS
                dve.wait_ge(s_max, (quad + 1) * (QUAD * T))
                wait(dve, s_maxT_psum, quad)
                dve.tensor_copy(max_parts[:, 0, :], maxima[:]).then_inc(s_split, 1)
                dve.wait_ge(s_split, n + 1)
                dve.tensor_tensor(max_rest[:], maxima[:], max_parts[:, 0, :], ALU.subtract).then_inc(s_split, 1)
                dve.wait_ge(s_split, n + 2)
                dve.tensor_copy(max_parts[:, 1, :], max_rest[:]).then_inc(s_split, 1)
                dve.wait_ge(s_split, n + 3)
                dve.tensor_tensor(max_rest2[:], max_rest[:], max_parts[:, 1, :], ALU.subtract).then_inc(s_split, 1)
                dve.wait_ge(s_split, n + 4)
                dve.tensor_copy(max_parts[:, 2, :], max_rest2[:]).then_inc(s_split, 1)

            def max_of(head, tiles):
                if head is None:
                    return
                i, s = head
                for t in tiles:
                    dve.wait_ge(s_scores, (i * H + s) * T + (t + 1))
                    if s % QUAD == 0 and t == 0:
                        wait(dve, s_split, (i * NQ + s // QUAD) * SPLIT_STEPS)
                    c = (s % QUAD) * T + t
                    dve.tensor_reduce(maxima[:, c:c + 1], scores[:, bank_of(s * T + t, NSC), :], AX_X, ALU.max)\
                       .then_inc(s_max, 1)
                    if c == QUAD * T - 1:
                        split_max(i * NQ + s // QUAD)

            def side_part(use):
                if use is None:
                    return
                name, arg, index, b = use
                which = name.split("_")[0]
                if name == "heads_T":
                    per_head = side[:, b, :].rearrange("p (t j c) -> p t j c", t=T, j=QUAD)
                    g = arg
                    dve.wait_ge(s_headsT, index + 1)
                    dve.reciprocal(sums_inv[:], per_head[:, :, :, DH]).then_inc(s_inv, 1)
                    dve.wait_ge(s_inv, index + 1)
                    dve.tensor_tensor(attn_out[:, :, g * QUAD:(g + 1) * QUAD, :], per_head[:, :, :, 0:DH],
                                      sums_inv[:].unsqueeze(3).to_broadcast([P, T, QUAD, DH]),
                                      ALU.mult).then_inc(s_attn, 1)
                elif name in ("ffn1_T", "ffn2_T"):
                    dve.wait_ge(s_hi[which], index + 1)
                    dve.tensor_tensor(x_lo[:], side[:, b, :], x_hi[:], ALU.subtract).then_inc(s_lo[which], 1)
                elif name == "v":
                    dve.wait_ge(s_v_psum, index + 1)
                    wait(dve, s_v_heads, index * NQ)
                    dve.tensor_tensor(v_next[:], side[:, b, :].rearrange("p (t d) -> p t d", t=T), rows[:, 0:1, :].to_broadcast([P, T, D]),
                                      ALU.add).then_inc(s_v_next, 1)
                elif name == "out":
                    dve.wait_ge(s_out_psum, index + 1)
                    dve.wait_ge(s_xb["out"], index + 1)
                    dve.tensor_tensor(batch_rows(index), side[:, b, :].rearrange("p (t d) -> p t d", t=T), xb["out"][:], ALU.add).then_inc(s_x2, 1)
                elif name.endswith("_down") and arg == T - 1:
                    dve.wait_ge(s_down[which], index + 1)
                    dve.wait_ge(s_xb[which], index + 1)
                    dve.tensor_tensor(batch_rows(index), side[:, b, :].rearrange("p (t d) -> p t d", t=T), xb[which][:], ALU.add)\
                       .then_inc(s_x1 if which == "ffn1" else s_y, 1)

            dve.memset(ones_f[:], 1.0).then_inc(s_ones, 1)
            dve.memset(minus_half[:], -0.5).then_inc(s_minus_half, 1)
            norm(("stats", "ffn1", 0))
            dve.wait_ge(s_ident, 16)
            dve.tensor_copy(ident_b[:], ident_f[:]).then_inc(s_ident_b, 1)
            dve.wait_ge(s_b2, 16)
            dve.tensor_scalar(b2_half[:], rows[:, 2:3, :], 0.5, None, ALU.mult).then_inc(s_b2h, 1)
            norm(("apply", "ffn1", 0))
            dve.wait_ge(s_gamma, 1)
            dve.tensor_scalar(thr[:, 0, :], side[:, 0, 0:2], 1.0 / (F * D), Q_EPS, ALU.mult, ALU.add).then_inc(s_thr, 1)
            dve.wait_ge(s_thr, 1)
            dve.tensor_scalar(thr[:, 1, :], thr[:, 0, :], 0.5, None, ALU.mult).then_inc(s_thr, 1)
            dve.tensor_scalar(thr[:, 2, :], thr[:, 0, :], -0.5, None, ALU.mult).then_inc(s_thr, 1)
            dve.wait_ge(s_thr, 3)
            dve.tensor_scalar(is_low[:], w1_raw[:], thr[:, 2, 0:1], None, ALU.is_lt).then_inc(s_thr, 1)
            dve.wait_ge(s_thr, 4)
            dve.scalar_tensor_tensor(out=w1_q[:], in0=w1_raw[:], scalar=thr[:, 1, 0:1], in1=is_low[:],
                                     op0=ALU.is_gt, op1=ALU.subtract).then_inc(s_wq, 1)
            side_part(PROLOGUE[0])
            dve.wait_ge(s_wq, 1)
            w2_flat = w2_raw[:].rearrange("p n d -> p (n d)")
            dve.tensor_scalar(is_low[:], w2_flat, thr[:, 2, 1:2], 0.5, ALU.is_lt, ALU.mult).then_inc(s_thr, 1)
            dve.tensor_scalar(is_high[:], w2_flat, thr[:, 1, 1:2], 0.5, ALU.is_gt, ALU.mult).then_inc(s_thr, 1)
            dve.wait_ge(s_thr, 6)
            dve.tensor_tensor(w2_q[:].rearrange("p n d -> p (n d)"), is_high[:], is_low[:], ALU.subtract).then_inc(s_wq, 1)
            for use in PROLOGUE[1:]:
                if use[0] == "v":
                    dve.wait_ge(s_const, 16 * CONST_DMAS)
                    rotate_begin(dve, "k", 0)
                side_part(use)
                if use[0] == "v":
                    rotate_end(dve, "dve", "k", 0)
                if use[:3] == ("ffn1_T", 0, 1):
                    rotate_begin(dve, "q", 0)
                    rotate_end(dve, "dve", "q", 0)
                if use[0] == "ffn1_down" and use[1] == T - 1:
                    norm(("stats", "attn", use[2]))
                    if use[2] == 0:
                        norm(("apply", "attn", 0))
                        norm(("stats", "ffn1", 1))
                        norm(("apply", "ffn1", 1))
            for s in range(LEAD):
                max_of((0, s), range(T))
                if s == 0:
                    norm(("apply", "attn", 1))
            for ph in phases(dve.Fori):
                i = ph.i
                for s in range(H):
                    ahead = ph.ahead(s)
                    max_of(ahead, (0,))
                    side_part(ph.side(s, 0))
                    norm(ph.ln(s, 0))
                    max_of(ahead, (1, 2))
                    side_part(ph.side(s, 1))
                    norm(ph.ln(s, 1))
                    max_of(ahead, (3,))
                    side_part(ph.side(s, 2))
                    norm(ph.ln(s, 2))

        @block.gpsimd
        def _(pool):
            def inv_std(n, j):
                pool.wait_ge(s_var[n], (j + 1) * T)
                alone(pool, "pool", s_normed[n], j * T)
                pool.tensor_scalar(var_eps[n][:], mean_var[n][:, :, 1], LN_EPS, None, ALU.add).then_inc(s_vareps[n], 1)
                pool.wait_ge(s_vareps[n], j + 1)
                pool.tensor_tensor(rstd[n][:], var_eps[n][:], minus_half[:], ALU.pow).then_inc(s_rstd[n], 1)

            def add_bias(n, j):
                ready, used, bias = {"ffn1": (None, s_x1, b2_half[:]), "out": (s_x1, s_x2, rows[:, 1:2, :]),
                                     "ffn2": (s_x2, s_y, b2_half[:])}[n]
                if ready is None:
                    pool.wait_ge(*((s_x0, 16) if isinstance(j, int) and j == 0 else (s_x, 16 * (B - 1))))
                else:
                    pool.wait_ge(ready, j + 1)
                alone(pool, "pool", used, j)
                pool.tensor_tensor(xb[n][:], batch_rows(j), bias.to_broadcast([P, T, D]), ALU.add).then_inc(s_xb[n], 1)

            def fill_values(j, g):
                pool.wait_ge(s_v_next, j + 1)
                alone(pool, "pool", s_pv, j * NQ + (g + 1 - NQ))
                pool.tensor_scalar(v_heads[:, :, g * QUAD:(g + 1) * QUAD, 0:DH],
                                   v_next[:].rearrange("p t (h c) -> p t h c", h=H)[:, :, g * QUAD:(g + 1) * QUAD, :],
                                   1.0, 0.0, ALU.mult, ALU.add).then_inc(s_v_heads, 1)

            pool.wait_ge(s_minus_half, 1)
            inv_std("ffn1", 0)
            pool.wait_ge(s_b2h, 1)
            add_bias("ffn1", 0)
            pool.memset(k_stack[:], -1.0).then_inc(s_k_fill, 1)
            pool.memset(v_heads[:], 0.0).then_inc(s_v_fill, 1)
            pool.wait_ge(s_v_fill, 1)
            pool.memset(v_heads[:, :, :, DH], 1.0).then_inc(s_v_fill, 1)
            inv_std("attn", 0)
            inv_std("ffn1", 1)
            add_bias("ffn1", 1)
            pool.wait_ge(s_v_fill, 2)
            fill_values(0, 0)
            fill_values(0, 1)
            inv_std("attn", 1)
            for ph in phases(pool.Fori):
                i = ph.i
                if ph.core:
                    fill_values(i, 2)
                if ph.post:
                    add_bias("out", i - 1)
                if ph.ffn1:
                    inv_std("ffn1", i + 2)
                if ph.proj:
                    rotate_begin(pool, "k", i + 1)
                    rotate_end(pool, "pool", "k", i + 1)
                if ph.core:
                    fill_values(i, 3)
                if ph.proj:
                    rotate_begin(pool, "q", i + 1)
                    rotate_end(pool, "pool", "q", i + 1)
                if ph.ffn1:
                    add_bias("ffn1", i + 2)
                if ph.post:
                    inv_std("ffn2", i - 1)
                    add_bias("ffn2", i - 1)
                if ph.ffn1:
                    inv_std("attn", i + 2)
                if ph.proj:
                    fill_values(i + 1, 0)
                    fill_values(i + 1, 1)


def kernel(**inputs):
    import concourse.bacc as bacc
    from concourse.bass_utils import run_bass_kernel_spmd

    def given(name, transpose=False):
        a = np.asarray(inputs[name])
        return np.ascontiguousarray(a.T if transpose else a)

    position = (np.arange(P)[None, :] * T + np.arange(T)[:, None]).reshape(-1).astype(np.float32)
    channel = np.arange(D) % DH
    inv_freq = (1.0 / np.float32(10000.0) ** (np.arange(0, DH, 2, dtype=np.float32) / np.float32(DH))).astype(np.float32)
    theta = (position[None, :] * inv_freq[channel // 2][:, None]).astype(np.float32)
    sign = np.where(channel % 2 == 0, -1.0, 1.0).astype(np.float32)[:, None]
    arrays = {
        "x": given("L0_attn_x"),
        "wq": given("L0_attn_Wq", True), "bq": given("L0_attn_bq").reshape(D, 1),
        "wk": given("L0_attn_Wk", True), "bk": given("L0_attn_bk").reshape(D, 1),
        "wv": given("L0_attn_Wv", True), "bv": given("L0_attn_bv"),
        "wo": given("L0_attn_Wo", True), "bo": given("L0_attn_bo"),
        "w1": given("L0_ffn_W1", True), "b1": np.ascontiguousarray(given("L0_ffn_b1").reshape(FT, P).T),
        "w2": given("L0_ffn_W2", True), "b2": given("L0_ffn_b2"),
        "ident": np.eye(P, dtype=np.float32),
        "rope_cos": np.cos(theta), "rope_sin": sign * np.sin(theta),
    }
    nc = bacc.Bacc("TRN2", target_bir_lowering=False, num_devices=1)
    args = [nc.dram_tensor(f"in_{n}", a.shape, mybir.dt.from_np(a.dtype), kind="ExternalInput").ap()
            for n, a in arrays.items()]
    out = nc.dram_tensor("out_y", (B, S, D), F32, kind="ExternalOutput").ap()
    macaron_layer(nc, *args, out)
    r = run_bass_kernel_spmd(nc, [{f"in_{n}": a for n, a in arrays.items()}], core_ids=[0])
    return r.results[0]["out_y"]
```
